# Optimizing a Trainium2 kernel written in Bass

```python
import numpy as np
import jax
import jax.numpy as jnp

def _softmax(x, axis=-1):
    return jax.nn.softmax(x, axis=axis)

def _gelu(x):
    return jax.nn.gelu(x, approximate=True)

def _silu(x):
    return jax.nn.silu(x)

def _sigmoid(x):
    return jax.nn.sigmoid(x)

def _layernorm(x, axis=-1, eps=1e-05):
    m = jnp.mean(x, axis=axis, keepdims=True)
    v = jnp.var(x, axis=axis, keepdims=True)
    return (x - m) / jnp.sqrt(v + eps)

def _scatter_add(tgt, idx, src, axis=0):
    return tgt.at[idx].add(src)

def _segment_sum(src, seg, n):
    return jax.ops.segment_sum(src, seg, n)
kernel_name = 'mk_adaln_ffn_d1_seqx_r2_4d28c3'

def setup_inputs(seed: int=0):
    np.random.seed(seed)
    _w = jnp.asarray

    def _rec_inputs():
        import jax
        import jax.numpy as jnp
        _rk = jax.random.key(seed)
        x = -0.000125 + 0.9999 * jax.random.normal(jax.random.fold_in(_rk, 1), (8, 512, 2048), jnp.float32)
        _lenS = 512 - jax.random.randint(jax.random.fold_in(_rk, 7), (8,), 0, max(1, 512 // 4) + 1, jnp.int32)
        _lenS2 = 512 - jax.random.randint(jax.random.fold_in(_rk, 8), (8,), 0, max(1, 512 // 4) + 1, jnp.int32)
        itok_B_1_7 = jax.random.randint(jax.random.fold_in(_rk, 11), (8,), 1, 8, jnp.int32)
        return (x, itok_B_1_7)
    x, itok_B_1_7 = _rec_inputs()

    def _L0_cond_setup():
        import jax, jax.numpy as jnp
        import numpy as np
        B, S, D_IN, D_OUT = (4, 1024, 2048, 2048)
        N_ADAPTERS, MAX_RANK = (8, 16)
        key = jax.random.key(seed)
        ks = jax.random.split(key, 7)
        x = jax.random.normal(ks[0], (B, S, D_IN), dtype=jnp.float32)
        weight = jax.random.normal(ks[1], (D_OUT, D_IN), dtype=jnp.float32) * (1.0 / np.sqrt(D_IN))
        bias = jax.random.normal(ks[2], (D_OUT,), dtype=jnp.float32) * 0.01
        lora_a_weights = jax.random.normal(ks[3], (N_ADAPTERS, MAX_RANK, D_IN), dtype=jnp.float32) * (1.0 / np.sqrt(D_IN))
        lora_b_weights = jax.random.normal(ks[4], (N_ADAPTERS, D_OUT, MAX_RANK), dtype=jnp.float32) * 0.02
        scaling_factors = jax.random.uniform(ks[5], (N_ADAPTERS,), dtype=jnp.float32, minval=0.5, maxval=2.0)
        adapter_id = jax.random.randint(ks[6], (B,), 0, N_ADAPTERS, dtype=jnp.int64)
        return {'x': x, 'weight': weight, 'bias': bias, 'lora_a_weights': lora_a_weights, 'lora_b_weights': lora_b_weights, 'scaling_factors': scaling_factors, 'adapter_id': adapter_id}
    _L0_cond_all = _L0_cond_setup()
    _L0_cond_in = {k: v for k, v in _L0_cond_all.items() if k in ('weight', 'bias', 'lora_a_weights', 'lora_b_weights', 'scaling_factors')}
    del _L0_cond_all

    def _L0_ffn_setup():
        import jax, jax.numpy as jnp
        import numpy as np
        NF4 = jnp.array([-1.0, -0.6961928009986877, -0.5250730514526367, -0.39491748809814453, -0.28444138169288635, -0.18477343022823334, -0.09105003625154495, 0.0, 0.07958029955625534, 0.16093020141124725, 0.24611230194568634, 0.33791524171829224, 0.44070982933044434, 0.5626170039176941, 0.7229568362236023, 1.0], dtype=jnp.float32)
        BLOCK = 64

        def _dequant_nf4(codes, absmax):
            vals = NF4[codes.reshape(-1)]
            w = vals.reshape(-1, BLOCK) * absmax[:, None]
            return w.reshape(codes.shape)
        key = jax.random.key(seed)
        k1, k2, k3, k4 = jax.random.split(key, 4)
        out_f, in_f = (2048, 2048)
        x = jax.random.normal(k1, (4, 1024, in_f), dtype=jnp.float32)
        codes = jax.random.randint(k2, (out_f, in_f), 0, 16, dtype=jnp.int32)
        absmax = jax.random.uniform(k3, (out_f * in_f // BLOCK,), dtype=jnp.float32)
        bias = jax.random.normal(k4, (out_f,), dtype=jnp.float32)
        return {'x': x, 'codes': codes, 'absmax': absmax, 'bias': bias}
    _L0_ffn_all = _L0_ffn_setup()
    _L0_ffn_in = {k: v for k, v in _L0_ffn_all.items() if k in ('codes', 'absmax', 'bias')}
    del _L0_ffn_all
    return {'x': x, 'itok_B_1_7': itok_B_1_7, 'L0_cond_weight': _L0_cond_in['weight'], 'L0_cond_bias': _L0_cond_in['bias'], 'L0_cond_lora_a_weights': _L0_cond_in['lora_a_weights'], 'L0_cond_lora_b_weights': _L0_cond_in['lora_b_weights'], 'L0_cond_scaling_factors': _L0_cond_in['scaling_factors'], 'L0_ffn_codes': _L0_ffn_in['codes'], 'L0_ffn_absmax': _L0_ffn_in['absmax'], 'L0_ffn_bias': _L0_ffn_in['bias']}

def reference(x, itok_B_1_7, L0_cond_weight, L0_cond_bias, L0_cond_lora_a_weights, L0_cond_lora_b_weights, L0_cond_scaling_factors, L0_ffn_codes, L0_ffn_absmax, L0_ffn_bias):
    import jax
    import jax.numpy as jnp

    def _L0_cond_ref(x, weight, bias, lora_a_weights, lora_b_weights, scaling_factors, adapter_id):
        import jax, jax.numpy as jnp
        import numpy as np
        B, S, D_IN, D_OUT = (4, 1024, 2048, 2048)
        N_ADAPTERS, MAX_RANK = (8, 16)
        base = jnp.einsum('bsi,oi->bso', x, weight) + bias
        a_sel = lora_a_weights[adapter_id]
        b_sel = lora_b_weights[adapter_id]
        scale = scaling_factors[adapter_id]
        low = jnp.einsum('bsi,bri->bsr', x, a_sel)
        delta = jnp.einsum('bsr,bor->bso', low, b_sel)
        return base + scale[:, None, None] * delta

    def _L0_ffn_ref(x, codes, absmax, bias):
        import jax, jax.numpy as jnp
        import numpy as np
        NF4 = jnp.array([-1.0, -0.6961928009986877, -0.5250730514526367, -0.39491748809814453, -0.28444138169288635, -0.18477343022823334, -0.09105003625154495, 0.0, 0.07958029955625534, 0.16093020141124725, 0.24611230194568634, 0.33791524171829224, 0.44070982933044434, 0.5626170039176941, 0.7229568362236023, 1.0], dtype=jnp.float32)
        BLOCK = 64

        def _dequant_nf4(codes, absmax):
            vals = NF4[codes.reshape(-1)]
            w = vals.reshape(-1, BLOCK) * absmax[:, None]
            return w.reshape(codes.shape)
        w = _dequant_nf4(codes, absmax)
        out = jnp.einsum('bsd,od->bso', x, w)
        return out + bias
    x = x + _L0_ffn_ref(_L0_cond_ref(x, L0_cond_weight, L0_cond_bias, L0_cond_lora_a_weights, L0_cond_lora_b_weights, L0_cond_scaling_factors, itok_B_1_7), L0_ffn_codes, L0_ffn_absmax, L0_ffn_bias)
    return x

_drawn_inputs = setup_inputs


def setup_inputs(seed=0):
    import zlib

    import numpy as np

    out = dict(_drawn_inputs(seed))
    spreads = {}
    factors = {'L0_cond_bias': 7.023}
    for name, (base, spread) in spreads.items():
        noise = np.random.default_rng([zlib.crc32(name.encode()), seed]).standard_normal(out[name].shape)
        drawn = base * np.exp(spread * noise) if base else spread * noise
        out[name] = jnp.asarray(drawn.astype(out[name].dtype))
    for name, factor in factors.items():
        out[name] = (out[name] * factor).astype(out[name].dtype)
    return out
```

```python
import numpy as np
import concourse.bass as bass
from concourse import mybir
from contextlib import ExitStack


def adaln_ffn_kernel(
    nc: bass.Bass,
    x: bass.AP,
    itok: bass.AP,
    weight: bass.AP,
    bias1: bass.AP,
    lora_a: bass.AP,
    lora_b: bass.AP,
    scaling: bass.AP,
    codes: bass.AP,
    absmax: bass.AP,
    bias2: bass.AP,
    identity: bass.AP,
    rank_of: bass.AP,
    adapter_of: bass.AP,
    restack: bass.AP,
    out: bass.AP,
):
    F32, F32R = mybir.dt.float32, mybir.dt.float32r
    I32, I16, BF16 = mybir.dt.int32, mybir.dt.int16, mybir.dt.bfloat16
    ALU, ACT = mybir.AluOpType, mybir.ActivationFunctionType
    P = 128
    NB, S, D = x.shape
    KT = D // P
    NA, R = lora_a.shape[0], lora_a.shape[1]
    QBLOCK = 64
    NQ = D // QBLOCK
    HI, LO = 0, 1

    NF4 = [-1.0, -0.6961928009986877, -0.5250730514526367, -0.39491748809814453, -0.28444138169288635,
           -0.18477343022823334, -0.09105003625154495, 0.0, 0.07958029955625534, 0.16093020141124725,
           0.24611230194568634, 0.33791524171829224, 0.44070982933044434, 0.5626170039176941,
           0.7229568362236023, 1.0]
    ZERO_CODE = 7
    STEP = 14
    LADDER = STEP << 7

    def rung(k):
        return float(np.float32(NF4[k])) * 2.0 ** (127 - STEP * abs(k - ZERO_CODE))

    CHUNKS = [256, 384, 384, 384, 384, 256]
    assert sum(CHUNKS) == D
    NCH = len(CHUNKS)
    O0 = [sum(CHUNKS[:c]) for c in range(NCH)]
    OT = [n // P for n in CHUNKS]
    WQ_COLS = max(CHUNKS)
    QD = 512
    NJ = D // QD
    UT = KT // NJ
    DT = QD // P
    PIECE0 = [NJ * sum(OT[:c]) for c in range(NCH + 1)]
    TILES = KT + 1
    G = TILES * NCH
    STEPS = KT + 2
    BUF0 = [[NJ * sum(1 for cc in range(c) if OT[cc] > u) for u in range(3)] for c in range(NCH + 1)]
    DEQ_OPS = 13

    HALVES, HO = 2, D // 2
    NO = HO // 512
    PT = 256
    PAIRS = NB * S // PT
    K_LORA = 3 * R + 4
    TURN = {t: ([2 * (t - 4), 2 * (t - 4) + 1] if t < 8 else [t]) for t in range(4, KT)}
    LOW_STEPS = range(1, 1 + KT // 2)
    RESTACK_STEP, LORA_STEP = 11, 14

    b_cols = nc.dram_tensor("b_cols", [D, NA * R], F32).ap()
    wt_d = nc.dram_tensor("wt_d", [KT, P, 2, D], F32).ap()
    a_sel_d = nc.dram_tensor("a_sel_d", [NB, P, KT * 2 * R], F32).ap()
    g_d = nc.dram_tensor("g_d", [NB, K_LORA, D], F32).ap()

    ctx = ExitStack()
    with ctx:
        sem = lambda name: ctx.enter_context(nc.semaphore(name))
        base = (nc.sbuf_base + 31) // 32 * 32
        KB = 1024

        def at(name, kb, shape, dt):
            return nc.alloc_sbuf_tensor_at(name, shape, dt, offset=base + int(kb * KB))

        wq_t = [at(f"wq_t{i}", 48 * i, [P, 2, KT, WQ_COLS], F32R) for i in range(2)]
        v_sb = at("v_sb", 96, [P, D], F32)
        bt_sb = at("bt_sb", 104, [2, D], F32)
        code_t = [at(f"code_t{i}", 112 + 2 * i, [P, QD], I32) for i in range(3)]
        ladder = [at(f"ladder{i}", 118 + 2 * i, [P, 2, QD], I16) for i in range(3)]
        w_nat = [at(f"w_nat{i}", 128 + 8 * i, [P, KT, P], F32) for i in range(2)]
        w_hl = [at(f"w_hl{i}", 144 + 16 * i, [P, 2, KT, P], F32R) for i in range(2)]
        deq = [at(f"deq{i}", 176 + 2 * i, [P, QD], F32) for i in range(4)]
        wq_nat = [at(f"wq_nat{i}", 184 + 2 * i, [P, QD], F32) for i in range(3)]
        wt_st = [at(f"wt_st{i}", 190 + 3 * i, [P, 2, WQ_COLS], F32) for i in range(2)]
        absm = at("absm", 196, [P, D // P, NQ], F32)
        a_nat = at("a_nat", 144, [P, D], F32)
        a_sel = at("a_sel", 152, [P, NB, KT, 2, R], F32)
        g_hl = [at(f"g_hl{i}", 64 + 8 * i, [P, D], F32) for i in range(2)]
        bt_hl = [at(f"bt_hl{i}", 80 + 8 * i, [2, D], F32) for i in range(2)]
        wt = at("wt", 0, [P, KT, 2, HO], F32R)
        x_nat = [at(f"x_nat{i}", 128 + 16 * i, [P, 2, D], F32) for i in range(2)]
        x_t = at("x_t", 160, [P, KT, 2, PT], F32R)
        a_b = at("a_b", 192, [P, KT, 2 * R], F32R)
        g_b = at("g_b", 194, [K_LORA, HO], F32R)
        o_st = [at(f"o_st{i}", 198 + 2 * i, [P, 512], F32) for i in range(2)]
        low_sb = at("low_sb", 202, [2 * R, PT], F32)
        low_st = at("low_st", 203, [K_LORA, PT], F32R)
        b1_nat = at("b1_nat", 204, [P, KT], F32)
        b1_hl = at("b1_hl", 204.0625, [P, KT, 2], F32R)
        ident = at("ident", 204.25, [P, P], F32)
        rst = at("rst", 204.75, [2 * R, 3 * R], F32)
        sel = at("sel", 205, [P, NB, R], F32)
        sel_s = at("sel_s", 205.5, [P, NB, R], F32)
        rank_c = at("rank_c", 206, [P, R], F32)
        adapt_c = at("adapt_c", 206.0625, [P, 1], F32)
        scale_c = at("scale_c", 206.09375, [P, 1], F32)
        ids_i = at("ids_i", 206.125, [P, NB], I32)
        ids_f = at("ids_f", 206.15625, [P, NB], F32)
        ids_w = at("ids_w", 206.1875, [P, NB], F32)
        hit = at("hit", 206.21875, [P, NB], F32)
        bias_l = at("bias_l", 206.25, [P, 1], F32)
        bias_h = at("bias_h", 206.28125, [P, 1], F32)
        bias2_sb = at("bias2_sb", 176, [1, D], F32)

        ps = [ctx.enter_context(nc.psum_tensor(f"ps{i}", [P, 512], F32)) for i in range(8)]
        acc1, tr1, a_ps = ps[0:2], ps[2:5], ps[5:7]
        acc2, rst_ps, tr2, low_ps = ps[0:4], ps[4], ps[5:7], ps[7]

        s_const = sem("const_loaded")
        s_small = sem("small_loaded")
        s_a_nat = sem("a_nat_loaded")
        s_bcols = sem("b_cols_stored")
        s_sel = sem("sel_chain")
        s_a_mm = sem("a_selected")
        s_a_hi = sem("a_hi_done")
        s_a_lo = sem("a_lo_done")
        s_a_st = sem("a_sel_stored")
        s_b1hi = sem("b1_hi_done")
        s_b1 = sem("b1_split")
        s_absm = sem("absmax_loaded")
        s_code = [sem(f"codes_loaded{i}") for i in range(3)]
        s_ladder = sem("ladder_made")
        s_dq = sem("dequantise_chain")
        s_piece = sem("piece_dequantised")
        s_tr1 = sem("piece_transposed")
        s_qhi = sem("wq_hi_done")
        s_qlo = sem("wq_lo_done")
        s_w = [sem(f"w_loaded{i}") for i in range(2)]
        s_whi = sem("w_hi_done")
        s_wlo = sem("w_lo_done")
        s_mm1 = sem("w_tile_multiplied")
        s_wthi = sem("wt_hi_done")
        s_evac1 = sem("acc1_evacuated")
        s_wtst = [sem(f"wt_stored{i}") for i in range(2)]
        s_gmm = sem("v_selected")
        s_bias2 = sem("bias2_loaded")
        s_btadd = sem("bt_added")
        s_ghi = sem("g_hi_done")
        s_glo = sem("g_lo_done")
        s_gst = sem("g_stored")
        s_wt = [sem(f"wt_loaded{k}") for k in range(KT)]
        s_x = [sem(f"x_loaded{i}") for i in range(2)]
        s_ab = sem("a_b_loaded")
        s_gb = sem("g_b_loaded")
        s_tr2 = sem("x_transposed")
        s_xhi = sem("x_hi_done")
        s_xlo = sem("x_lo_done")
        s_step = sem("steps_done")
        s_low = sem("low_done")
        s_lowev = sem("low_evacuated")
        s_rst = sem("low_restacked")
        s_lsthi = sem("low_stack_hi")
        s_lstone = sem("low_stack_ones")
        s_lst = sem("low_stack_done")
        s_lora = sem("lora_added")
        s_acc = sem("acc2_done")
        s_evac2 = sem("acc2_evacuated")
        s_ost = [sem(f"out_stored{i}") for i in range(2)]

        block = ctx.enter_context(nc.Block())

        def piece_at(c, j, u, ahead):
            u += ahead
            while c < NCH and u >= OT[c]:
                u -= OT[c]
                if isinstance(j, int) and j == NJ - 1:
                    c, j = c + 1, 0
                else:
                    j = j + 1
            return (c, j, u) if c < NCH else None

        def number(c, j, u):
            return PIECE0[c] + u + j * OT[c]

        def wqt_part(c, hl, j, u):
            t = wq_t[c % 2]
            return t[:, hl, bass.ds(j * DT, DT), u * P:(u + 1) * P]

        @block.sync
        def _(sp):
            def load_codes(c, j, u):
                sp.wait_ge(s_ladder, number(c, j, u) + 1)
                row = O0[c] + u * P
                sp.dma_start(code_t[u][:, :], codes[row:row + P, bass.ds(j * QD, QD)]).then_inc(s_code[u], 16)

            def load_tile(c, s_static, s, src):
                g0 = TILES * c + s_static
                g = TILES * c + s
                sp.wait_ge(s_wlo, 2 * g + 2)
                sp.dma_start(w_nat[g0 % 2][:, :, :], src).then_inc(s_w[g0 % 2], 16)

            def w_src(s):
                return weight.rearrange("(t p) i -> p t i", p=P)[:, :, bass.ds(s * P, P)]

            b_src = b_cols.rearrange("(t p) r -> p t r", p=P)

            def store_wt(c, s_static, s):
                sp.wait_ge(s_evac1, 2 + STEPS * c + s + 1)
                n = CHUNKS[c]
                dst = wt_d.rearrange("k p h o -> p k h o")[:, bass.ds(s, 1), :, O0[c]:O0[c] + n].rearrange(
                    "p k h o -> p (k h) o")
                sp.dma_start(dst, wt_st[s_static % 2][:, :, 0:n]).then_inc(s_wtst[s_static % 2], 16)

            sp.sem_inc(s_wtst[0], 16)
            sp.sem_inc(s_wtst[1], 16)
            load_codes(0, 0, 0)
            load_codes(0, 0, 1)
            sp.dma_start(absm[:, :, :], absmax.rearrange("(t p b) -> p t b", p=P, b=NQ)).then_inc(s_absm, 16)
            sp.dma_start(ids_i[:, :], itok.partition_broadcast(P)).then_inc(s_small, 16)
            sp.dma_start(scale_c[:, :], bass.AP(scaling.tensor, scaling.offset, [[1, NA], [0, R], [1, 1]])
                         ).then_inc(s_small, 16)
            sp.dma_start(rank_c[:, :], rank_of).then_inc(s_const, 16)
            sp.dma_start(adapt_c[:, :], adapter_of).then_inc(s_const, 16)
            sp.dma_start(ident[:, :], identity).then_inc(s_const, 16)
            sp.dma_start(rst[:, :], restack).then_inc(s_const, 16)
            sp.dma_start(a_nat[:, :], lora_a.rearrange("a r i -> (a r) i")).then_inc(s_a_nat, 16)
            sp.dma_start(b1_nat[:, :], bias1.rearrange("(t p) -> p t", p=P),
                         allow_slow_non_contiguous=True).then_inc(s_small, 16)
            load_tile(0, 0, 0, w_src(0))
            load_tile(0, 1, 1, w_src(1))
            for j in range(NJ):
                for u in range(OT[0]):
                    load_codes(*piece_at(0, j, u, 2))
            for a in range(NA):
                sp.dma_start(b_cols[:, a * R:(a + 1) * R], lora_b[a]).then_inc(s_bcols, 16)
            sp.wait_ge(s_a_hi, 4)
            sp.wait_ge(s_a_lo, 4)
            sp.dma_start(a_sel_d.rearrange("b p f -> p b f"),
                         a_sel[:, :, :, :, :].rearrange("p b k h r -> p b (k h r)")).then_inc(s_a_st, 16)

            for c in range(NCH):
                def step(j, u):
                    s = j * UT + u
                    static = isinstance(j, int)
                    if not (static and s < 2 and c == 0):
                        load_tile(c, u, s, w_src(s))
                    if static and s == 1 and c:
                        store_wt(c - 1, KT - 1, KT - 1)
                    if not static or s >= 3:
                        store_wt(c, u + 1, s - 3)
                    if c + 1 < NCH and u < OT[c + 1]:
                        nxt = piece_at(c + 1, j, u, 2)
                        if nxt:
                            load_codes(*nxt)

                for u in range(UT):
                    step(0, u)
                with sp.Fori(1, NJ - 1) as j:
                    for u in range(UT):
                        step(j, u)
                for u in range(UT):
                    step(NJ - 1, u)
                if c == 0:
                    sp.wait_ge(s_bcols, 16 * NA)
                load_tile(c, KT, KT, b_src)
                store_wt(c, (KT - 3) % 2, KT - 3)
                store_wt(c, (KT - 2) % 2, KT - 2)
            store_wt(NCH - 1, KT - 1, KT - 1)
            sp.wait_ge(s_piece, 2 + PIECE0[NCH])
            sp.dma_start(bias2_sb[:, :], bias2.rearrange("(a o) -> a o", a=1)).then_inc(s_bias2, 16)

            sp.wait_ge(s_mm1, STEPS * NCH)
            sp.wait_ge(s_evac1, 2 + STEPS * NCH)
            x_p = x.rearrange("b (q u p) d -> (b q) p u d", u=2, p=P)
            o_p = out.rearrange("b (q u p) d -> (b q) p u d", u=2, p=P)

            def pair(ap, pp):
                return ap.rearrange("n p u d -> p n u d")[:, bass.ds(pp, 1), :, :].rearrange("p n u d -> p (n u) d")

            def load_x(par, pp):
                sp.dma_start(x_nat[par][:, :, :], pair(x_p, pp)).then_inc(s_x[par], 16)

            def load_a(b):
                src = a_sel_d.rearrange("b p f -> p b f")[:, bass.ds(b, 1), :].rearrange("p b f -> p (b f)")
                sp.dma_start(a_b[:, :, :].rearrange("p k r -> p (k r)").bitcast(F32), src).then_inc(s_ab, 16)

            def load_g(h, b):
                src = g_d.rearrange("b k o -> k b o")[:, bass.ds(b, 1), h * HO:(h + 1) * HO].rearrange(
                    "k b o -> k (b o)")
                sp.dma_start(g_b[:, :].bitcast(F32), src).then_inc(s_gb, 16)

            sp.wait_ge(s_wtst[0], 16 * (1 + NCH * KT // 2))
            sp.wait_ge(s_wtst[1], 16 * (1 + NCH * KT // 2))
            load_x(0, 0)
            load_x(1, 1)
            sp.wait_ge(s_a_st, 16)
            load_a(0)
            sp.wait_ge(s_ghi, 5)
            sp.wait_ge(s_glo, 5)
            for b in range(NB):
                rows = slice(b * R, (b + 1) * R)
                sp.dma_start(g_d[b, 0:R, :], g_hl[HI][rows, :]).then_inc(s_gst, 16)
                sp.dma_start(g_d[b, R:2 * R, :], g_hl[LO][rows, :]).then_inc(s_gst, 16)
                sp.dma_start(g_d[b, 2 * R:3 * R, :], g_hl[HI][rows, :]).then_inc(s_gst, 16)
                sp.dma_start(g_d[b, 3 * R:3 * R + 2, :], bt_hl[HI][:, :]).then_inc(s_gst, 16)
                sp.dma_start(g_d[b, 3 * R + 2:3 * R + 4, :], bt_hl[LO][:, :]).then_inc(s_gst, 16)
            sp.wait_ge(s_gst, 16 * 5 * NB)
            load_g(0, 0)

            sp.sem_inc(s_ost[0], 16)
            sp.sem_inc(s_ost[1], 16)

            def store_pair(h, b, w):
                pp = (h * NB + b) * 2 + w
                for k in range(2 * NO):
                    sp.wait_ge(s_evac2, 4 + 4 * pp + k + 1)
                    col = h * HO + (k % NO) * 512
                    dst = pair(o_p, 2 * b + w)[:, k // NO, col:col + 512]
                    sp.dma_start(dst, o_st[k % 2][:, :]).then_inc(s_ost[k % 2], 16)

            def batch(h, b, following):
                v = h * NB + b
                store_pair(h, b, 0)
                if following:
                    load_x(0, 2 * following[1])
                    sp.wait_ge(s_low, 2 * v + 2)
                    load_a(following[1])
                    sp.wait_ge(s_lora, 2 * v + 2)
                    load_g(*following)
                store_pair(h, b, 1)
                if following:
                    load_x(1, 2 * following[1] + 1)

            for h in range(HALVES):
                with sp.Fori(0, NB - 1) as b:
                    batch(h, b, (h, b + 1))
                batch(h, NB - 1, (h + 1, 0) if h + 1 < HALVES else None)
            for i in range(2):
                sp.wait_ge(s_ost[i], 16 * (1 + HALVES * PAIRS * NO))

        @block.gpsimd
        def _(pool):
            def split_lo(c, u, s, half):
                g0, g = TILES * c + u, TILES * c + s
                par, rows = g0 % 2, slice(half * KT // 2, (half + 1) * KT // 2)
                pool.wait_ge(s_whi, 2 * g + half + 1)
                nc.gpsimd.tensor_tensor(w_hl[par][:, LO, rows, :], w_nat[par][:, rows, :],
                                        w_hl[par][:, HI, rows, :].bitcast(F32), ALU.subtract).then_inc(s_wlo, 1)

            pool.sem_inc(s_wlo, 4)
            for c in range(NCH):
                with pool.Fori(0, NJ) as j:
                    for u in range(UT):
                        for half in range(2):
                            split_lo(c, u, j * UT + u, half)
                for half in range(2):
                    split_lo(c, KT, KT, half)

            def load_wt(h, k):
                pool.dma_start(wt[:, k, :, :].bitcast(F32), wt_d[k, :, :, h * HO:(h + 1) * HO]
                               ).then_inc(s_wt[k], 16)

            pool.wait_ge(s_mm1, STEPS * NCH)
            pool.wait_ge(s_wtst[0], 16 * (1 + NCH * KT // 2))
            pool.wait_ge(s_wtst[1], 16 * (1 + NCH * KT // 2))
            for k in range(KT):
                if k == KT // 2:
                    pool.wait_ge(s_gst, 16 * 5 * NB)
                load_wt(0, k)
            for h in range(1, HALVES):
                for k in range(KT):
                    if k < KT - 1:
                        pool.wait_ge(s_step, (h * PAIRS - 1) * (KT - 1) + k + 1)
                    else:
                        pool.wait_ge(s_acc, h * PAIRS * 2 * NO)
                    load_wt(h, k)

        @block.scalar
        def _(act):
            def make_ladders(c, j, u):
                cnt = BUF0[c][u] + j
                act.wait_ge(s_code[u], 16 * (cnt + 1))
                act.wait_ge(s_piece, number(c, j, u) + 1)
                nc.scalar.activation(ladder[u][:, 0, :], code_t[u][:, :], ACT.Relu, bias=bias_l[:, 0:1],
                                     scale=float(LADDER))
                nc.scalar.activation(ladder[u][:, 1, :], code_t[u][:, :], ACT.Relu, bias=bias_h[:, 0:1],
                                     scale=-float(LADDER)).then_inc(s_ladder, 1)

            def piece_hi(c, j, u):
                act.wait_ge(s_tr1, 2 + number(c, j, u) + 1)
                nc.scalar.copy(wqt_part(c, HI, j, u), tr1[u][:, :].rearrange("p (t o) -> p t o", t=DT)
                               ).then_inc(s_qhi, 1)

            def split_hi(g0, g):
                par = g0 % 2
                act.wait_ge(s_w[par], 16 * (g0 // 2 + 1) + 8 * (g - g0))
                for half in range(2):
                    rows = slice(half * KT // 2, (half + 1) * KT // 2)
                    nc.scalar.copy(w_hl[par][:, HI, rows, :], w_nat[par][:, rows, :]).then_inc(s_whi, 1)

            def evacuate_hi(c, u, s):
                n = CHUNKS[c]
                q = KT // 2 * c
                act.wait_ge(s_wtst[u % 2], 16 * (1 + q + (s - u) // 2 + u // 2) if isinstance(s, int)
                            else 16 * (1 + q + u // 2) + 8 * (s - u))
                nc.scalar.copy(wt_st[u % 2][:, HI, 0:n].bitcast(F32R), acc1[u % 2][:, 0:n]).then_inc(s_wthi, 1)

            act.wait_ge(s_sel, 2)
            make_ladders(0, 0, 0)
            make_ladders(0, 0, 1)
            act.wait_ge(s_small, 48)
            nc.scalar.copy(b1_hl[:, :, HI], b1_nat[:, :]).then_inc(s_b1hi, 1)

            def piece_step(c, j, u):
                nxt = piece_at(c, j, u, 2)
                if nxt:
                    make_ladders(*nxt)
                piece_hi(c, j, u)

            for q in range(4):
                act.wait_ge(s_a_mm, q + 1)
                dst = a_sel[:, :, q * 4:(q + 1) * 4, HI, :].bitcast(F32R).rearrange("p b k r -> p k b r")
                nc.scalar.copy(dst, a_ps[q % 2][:, :].rearrange("p (k b r) -> p k b r", k=4, b=NB)
                               ).then_inc(s_a_hi, 1)
            for j in range(NJ):
                for u in range(OT[0]):
                    piece_step(0, j, u)
            act.wait_ge(s_a_st, 16)
            split_hi(0, 0)
            split_hi(1, 1)
            for c in range(NCH):
                def step(j, u):
                    s = j * UT + u
                    g0, g = TILES * c + u, TILES * c + s
                    act.wait_ge(s_mm1, STEPS * c + s + 1)
                    if not (isinstance(s, int) and g + 2 >= G):
                        split_hi(g0 + 2, g + 2)
                    if c + 1 < NCH and u < OT[c + 1]:
                        piece_step(c + 1, j, u)
                    evacuate_hi(c, u, s)

                with act.Fori(0, NJ - 1) as j:
                    for u in range(UT):
                        step(j, u)
                for u in range(UT):
                    step(NJ - 1, u)
                if c + 1 < NCH:
                    act.wait_ge(s_mm1, STEPS * c + KT + 1)
                    split_hi(TILES * c + KT + 2, TILES * c + KT + 2)

            act.wait_ge(s_btadd, 1)
            nc.scalar.copy(bt_hl[HI][:, :].bitcast(F32R), bt_sb[:, :]).then_inc(s_ghi, 1)
            for q in range(4):
                act.wait_ge(s_gmm, q + 1)
                nc.scalar.copy(g_hl[HI][:, q * 512:(q + 1) * 512].bitcast(F32R), ps[q][:, :]).then_inc(s_ghi, 1)

            def slot_hi(pp, j):
                act.wait_ge(s_tr2, pp * KT + j + 1)
                nc.scalar.copy(x_t[:, j, HI, :], tr2[j % 2][:, 0:PT]).then_inc(s_xhi, 1)

            for j in range(KT):
                slot_hi(0, j)

            def pair_hi(pp, more):
                for t in range(KT):
                    if t == LOW_STEPS[-1]:
                        act.wait_ge(s_low, pp + 1)
                        nc.scalar.copy(low_sb[:, :], low_ps[0:2 * R, 0:PT]).then_inc(s_lowev, 1)
                    if t == RESTACK_STEP:
                        act.wait_ge(s_rst, pp + 1)
                        nc.scalar.copy(low_st[0:3 * R, :], rst_ps[0:3 * R, 0:PT]).then_inc(s_lsthi, 1)
                    if more:
                        for j in TURN.get(t, ()):
                            slot_hi(pp + 1, j)

            act.wait_ge(s_lstone, 1)
            with act.Fori(0, NB * HALVES - 1) as b:
                pair_hi(2 * b, True)
                pair_hi(2 * b + 1, True)
            pair_hi(HALVES * PAIRS - 2, True)
            pair_hi(HALVES * PAIRS - 1, False)

        @block.vector
        def _(dve):
            count = [0]

            def link(ins):
                count[0] += 1
                ins.then_inc(s_sel, 1)
                dve.wait_ge(s_sel, count[0])

            dve.sem_inc(s_ladder, 2)
            dve.sem_inc(s_piece, 2)
            dve.sem_inc(s_tr1, 2)
            dve.sem_inc(s_qlo, 2)
            dve.sem_inc(s_evac1, 2)
            link(nc.vector.memset(bias_l[:, :], -float(ZERO_CODE * LADDER)))
            link(nc.vector.memset(bias_h[:, :], float(ZERO_CODE * LADDER)))
            dve.wait_ge(s_small, 48)
            dve.wait_ge(s_const, 64)
            link(nc.vector.tensor_copy(ids_f[:, :], ids_i[:, :]))
            link(nc.vector.tensor_scalar(ids_w[:, :], ids_f[:, :], 0.0, float(NA), ALU.is_lt, ALU.mult))
            link(nc.vector.tensor_tensor(ids_w[:, :], ids_w[:, :], ids_f[:, :], ALU.add))
            link(nc.vector.tensor_scalar(ids_w[:, :], ids_w[:, :], 0.0, float(NA - 1), ALU.max, ALU.min))
            link(nc.vector.tensor_scalar(hit[:, :], ids_w[:, :], adapt_c[:, 0:1], None, ALU.is_equal))
            link(nc.vector.tensor_tensor(sel[:, :, :], hit[:, :].unsqueeze(2).to_broadcast([P, NB, R]),
                                         rank_c[:, :].unsqueeze(1).to_broadcast([P, NB, R]), ALU.mult))
            link(nc.vector.tensor_scalar(sel_s[:, :, :], sel[:, :, :], scale_c[:, 0:1], None, ALU.mult))
            dve.wait_ge(s_b1hi, 1)
            nc.vector.tensor_tensor(b1_hl[:, :, LO], b1_nat[:, :], b1_hl[:, :, HI].bitcast(F32),
                                    ALU.subtract).then_inc(s_b1, 1)

            def dequantise(c, j, u):
                n = number(c, j, u)
                up = ladder[u][:, 0, :].bitcast(BF16)
                down = ladder[u][:, 1, :].bitcast(BF16)
                a, b, e, d = (t[:, :] for t in deq)
                V = [float(np.float32(v)) for v in NF4]
                ts, tt, stt = nc.vector.tensor_scalar, nc.vector.tensor_tensor, nc.vector.scalar_tensor_tensor

                def after(k):
                    dve.wait_ge(s_dq, n * DEQ_OPS + k + 1)

                def tell(ins):
                    ins.then_inc(s_dq, 1)

                dve.wait_ge(s_ladder, 2 + n + 1)
                dve.wait_ge(s_piece, 2 + n)
                tell(ts(a, up, rung(14), V[13], ALU.mult, ALU.max))
                tell(ts(b, up, rung(12), V[11], ALU.mult, ALU.max))
                tell(ts(e, down, rung(0), V[1], ALU.mult, ALU.min))
                tell(ts(d, down, rung(2), V[3], ALU.mult, ALU.min))
                after(1)
                tell(stt(a, a, V[15], b, ALU.min, ALU.min))
                after(3)
                tell(tt(e, e, d, ALU.max))
                after(4)
                tell(ts(b, up, rung(10), V[9], ALU.mult, ALU.max))
                after(5)
                tell(ts(d, down, rung(4), V[5], ALU.mult, ALU.min))
                after(6)
                tell(tt(a, a, b, ALU.min))
                after(7)
                tell(tt(e, e, d, ALU.max))
                after(9)
                tell(stt(e, down, rung(6), e, ALU.mult, ALU.max))
                after(10)
                tell(stt(e, up, rung(8), e, ALU.mult, ALU.add))
                after(11)
                tell(tt(a, a, e, ALU.min))
                after(12)
                dve.wait_ge(s_tr1, n + 1)
                tt(wq_nat[u][:, :].rearrange("p (q e) -> p q e", e=QBLOCK),
                   a.rearrange("p (q e) -> p q e", e=QBLOCK),
                   absm[:, O0[c] // P + u, bass.ds(j * (QD // QBLOCK), QD // QBLOCK)].unsqueeze(2)
                   .to_broadcast([P, QD // QBLOCK, QBLOCK]), ALU.mult).then_inc(s_piece, 1)

            def piece_lo(c, j, u):
                dve.wait_ge(s_qhi, number(c, j, u) + 1)
                hi = wqt_part(c, HI, j, u)
                nc.vector.tensor_tensor(wqt_part(c, LO, j, u), tr1[u][:, :].rearrange("p (t o) -> p t o", t=DT),
                                        hi.bitcast(F32), ALU.subtract).then_inc(s_qlo, 1)

            def piece_step(c, j, u):
                nxt = piece_at(c, j, u, 1)
                if nxt:
                    dequantise(*nxt)
                piece_lo(c, j, u)

            dve.wait_ge(s_absm, 16)
            dequantise(0, 0, 0)
            for q in range(4):
                dve.wait_ge(s_a_hi, q + 1)
                nc.vector.tensor_tensor(a_sel[:, :, q * 4:(q + 1) * 4, LO, :].rearrange("p b k r -> p k b r"),
                                        a_ps[q % 2][:, :].rearrange("p (k b r) -> p k b r", k=4, b=NB),
                                        a_sel[:, :, q * 4:(q + 1) * 4, HI, :].rearrange("p b k r -> p k b r"),
                                        ALU.subtract).then_inc(s_a_lo, 1)
            for j in range(NJ):
                for u in range(OT[0]):
                    piece_step(0, j, u)
            for c in range(NCH):
                def step(j, u):
                    s = j * UT + u
                    n = CHUNKS[c]
                    if c + 1 < NCH and u < OT[c + 1]:
                        piece_step(c + 1, j, u)
                    dve.wait_ge(s_wthi, KT * c + s + 1)
                    nc.vector.tensor_tensor(wt_st[u % 2][:, LO, 0:n], acc1[u % 2][:, 0:n],
                                            wt_st[u % 2][:, HI, 0:n], ALU.subtract).then_inc(s_evac1, 1)

                with dve.Fori(0, NJ - 1) as j:
                    for u in range(UT):
                        step(j, u)
                for u in range(UT):
                    step(NJ - 1, u)
                n = CHUNKS[c]
                dve.wait_ge(s_mm1, STEPS * c + KT + 1)
                nc.vector.tensor_copy(v_sb[:, O0[c]:O0[c] + n], acc1[KT % 2][:, 0:n]).then_inc(s_evac1, 1)
                dve.wait_ge(s_mm1, STEPS * c + KT + 2)
                nc.vector.tensor_copy(bt_sb[:, O0[c]:O0[c] + n], acc1[(KT + 1) % 2][0:2, 0:n]).then_inc(s_evac1, 1)

            dve.wait_ge(s_bias2, 16)
            dve.wait_ge(s_evac1, 2 + STEPS * NCH)
            nc.vector.tensor_tensor(bt_sb[0:1, :], bt_sb[0:1, :], bias2_sb[:, :], ALU.add).then_inc(s_btadd, 1)
            dve.wait_ge(s_btadd, 1)
            dve.wait_ge(s_ghi, 1)
            nc.vector.tensor_tensor(bt_hl[LO][:, :], bt_sb[:, :], bt_hl[HI][:, :], ALU.subtract).then_inc(s_glo, 1)
            for q in range(4):
                cols = slice(q * 512, (q + 1) * 512)
                dve.wait_ge(s_ghi, q + 2)
                nc.vector.tensor_tensor(g_hl[LO][:, cols], ps[q][:, :], g_hl[HI][:, cols],
                                        ALU.subtract).then_inc(s_glo, 1)

            dve.sem_inc(s_xlo, 2)
            dve.sem_inc(s_evac2, 4)
            nc.vector.memset(low_st[:, :].bitcast(F32), 1.0).then_inc(s_lstone, 1)

            def slot_lo(pp, j):
                dve.wait_ge(s_xhi, pp * KT + j + 1)
                nc.vector.tensor_tensor(x_t[:, j, LO, :], tr2[j % 2][:, 0:PT], x_t[:, j, HI, :].bitcast(F32),
                                        ALU.subtract).then_inc(s_xlo, 1)

            for j in range(KT):
                slot_lo(0, j)

            def pair_lo(h, b, w, more):
                pp = (h * NB + b) * 2 + w
                for t in range(KT):
                    if t == KT - 1:
                        for k in range(2 * NO):
                            u, q = divmod(k, NO)
                            dve.wait_ge(s_acc, 4 * pp + k + 1)
                            dve.wait_ge(s_ost[k % 2], 16 * (2 * pp + k // 2 + 1))
                            col = h * HO + q * 512
                            nc.vector.tensor_tensor(o_st[k % 2][:, :], acc2[k][:, :],
                                                    x_nat[w][:, u, col:col + 512], ALU.add).then_inc(s_evac2, 1)
                    if t == RESTACK_STEP:
                        dve.wait_ge(s_lsthi, pp + 1)
                        rows = slice(2 * R, 3 * R)
                        nc.vector.tensor_tensor(low_st[rows, :], rst_ps[rows, 0:PT],
                                                low_st[rows, :].bitcast(F32), ALU.subtract).then_inc(s_lst, 1)
                    if more:
                        for j in TURN.get(t, ()):
                            slot_lo(pp + 1, j)

            for h in range(HALVES):
                last = h + 1 == HALVES
                with dve.Fori(0, NB - last) as b:
                    pair_lo(h, b, 0, True)
                    pair_lo(h, b, 1, True)
                if last:
                    pair_lo(h, NB - 1, 0, True)
                    pair_lo(h, NB - 1, 1, False)

        @block.tensor
        def _(pe):
            pe.wait_ge(s_a_nat, 16)
            pe.wait_ge(s_const, 64)
            pe.wait_ge(s_sel, 9)
            for q in range(4):
                if q >= 2:
                    pe.wait_ge(s_a_lo, q - 1)
                for t in range(4):
                    i = 4 * q + t
                    last = nc.tensor.matmul(a_ps[q % 2][:, t * P:(t + 1) * P], a_nat[:, i * P:(i + 1) * P],
                                            sel[:, :, :].rearrange("p b r -> p (b r)"), start=True, stop=True)
                last.then_inc(s_a_mm, 1)

            def transpose_piece(c, j, u):
                n = number(c, j, u)
                pe.wait_ge(s_piece, 2 + n + 1)
                pe.wait_ge(s_qlo, n + 1)
                for t in range(DT):
                    last = nc.tensor.transpose(tr1[u][:, t * P:(t + 1) * P], wq_nat[u][:, t * P:(t + 1) * P],
                                               ident[:, :])
                last.then_inc(s_tr1, 1)

            def three(out_ap, hi_t, lo_t, hi_m, lo_m, first, last):
                nc.tensor.matmul(out_ap, hi_t, hi_m, start=first, stop=False)
                nc.tensor.matmul(out_ap, hi_t, lo_m, start=False, stop=False)
                return nc.tensor.matmul(out_ap, lo_t, hi_m, start=False, stop=last)

            for j in range(NJ):
                for u in range(OT[0]):
                    transpose_piece(0, j, u)
            pe.wait_ge(s_b1, 1)
            for c in range(NCH):
                n = CHUNKS[c]
                wq = wq_t[c % 2]
                pe.wait_ge(s_qlo, 2 + PIECE0[c + 1])

                def tile_products(u, s):
                    par = (TILES * c + u) % 2
                    pe.wait_ge(s_wlo, 4 + 2 * (TILES * c + s) + 2)
                    pe.wait_ge(s_evac1, STEPS * c + s + 1)
                    t = w_hl[par]
                    for k in range(KT):
                        last = three(acc1[u % 2][:, 0:n], t[:, HI, k, :], t[:, LO, k, :],
                                     wq[:, HI, k, 0:n], wq[:, LO, k, 0:n], k == 0, k == KT - 1)
                    last.then_inc(s_mm1, 1)

                with pe.Fori(0, NJ) as j:
                    for u in range(UT):
                        tile_products(u, j * UT + u)
                        if c + 1 < NCH and u < OT[c + 1]:
                            transpose_piece(c + 1, j, u)
                tile_products(KT, KT)
                pe.wait_ge(s_evac1, STEPS * c + KT + 2)
                for k in range(KT):
                    nc.tensor.matmul(acc1[1][0:2, 0:n], b1_hl[:, k, :], wq[:, HI, k, 0:n],
                                     start=(k == 0), stop=False)
                    last = nc.tensor.matmul(acc1[1][0:2, 0:n], b1_hl[:, k, :], wq[:, LO, k, 0:n],
                                            start=False, stop=(k == KT - 1))
                last.then_inc(s_mm1, 1)

            pe.wait_ge(s_evac1, 2 + STEPS * NCH)
            for q in range(4):
                nc.tensor.matmul(ps[q][:, :], sel_s[:, :, :].rearrange("p b r -> p (b r)"),
                                 v_sb[:, q * 512:(q + 1) * 512], start=True, stop=True).then_inc(s_gmm, 1)

            def transpose_slot(pp, w, j):
                pe.wait_ge(s_xlo, pp * KT + j + 1)
                for u in range(2):
                    last = nc.tensor.transpose(tr2[j % 2][:, u * P:(u + 1) * P], x_nat[w][:, u, j * P:(j + 1) * P],
                                               ident[:, :])
                last.then_inc(s_tr2, 1)

            pe.wait_ge(s_x[0], 16)
            for j in range(KT):
                transpose_slot(0, 0, j)

            def pair_products(h, b, w, more):
                v = h * NB + b
                pp = 2 * v + w
                for t in range(KT):
                    pe.wait_ge(s_xlo, 2 + pp * KT + t + 1)
                    pe.wait_ge(s_wt[t], 16 * (h + 1))
                    for k in range(2 * NO):
                        u, q = divmod(k, NO)
                        if t == 0:
                            pe.wait_ge(s_evac2, 4 * pp + k + 1)
                            if h == 0 and k == 0 and w == 0:
                                pe.wait_ge(s_glo, 5)
                        tok, cols = slice(u * P, (u + 1) * P), slice(q * 512, (q + 1) * 512)
                        last = three(acc2[k][:, :], x_t[:, t, HI, tok], x_t[:, t, LO, tok],
                                     wt[:, t, HI, cols], wt[:, t, LO, cols], t == 0, t == KT - 1)
                        if t == KT - 1:
                            last.then_inc(s_acc, 1)
                    if t < KT - 1:
                        last.then_inc(s_step, 1)
                    if t in LOW_STEPS:
                        if t == LOW_STEPS[0]:
                            pe.wait_ge(s_ab, 16 * (v + 1))
                        for j in (2 * (t - 1), 2 * (t - 1) + 1):
                            pe.wait_ge(s_xlo, 2 + pp * KT + j + 1)
                            for hl in (HI, LO):
                                last = nc.tensor.matmul(low_ps[0:2 * R, 0:PT], a_b[:, j, :], x_t[:, j, hl, :],
                                                        start=(j == 0 and hl == HI),
                                                        stop=(j == KT - 1 and hl == LO))
                        if t == LOW_STEPS[-1]:
                            last.then_inc(s_low, 1)
                    if t == RESTACK_STEP:
                        pe.wait_ge(s_lowev, pp + 1)
                        nc.tensor.matmul(rst_ps[0:3 * R, 0:PT], rst[:, :], low_sb[:, :], start=True,
                                         stop=True).then_inc(s_rst, 1)
                    if t == LORA_STEP:
                        pe.wait_ge(s_lst, pp + 1)
                        pe.wait_ge(s_gb, 16 * (v + 1))
                        for k in range(2 * NO):
                            u, q = divmod(k, NO)
                            last = nc.tensor.matmul(acc2[k][:, :], low_st[:, u * P:(u + 1) * P],
                                                    g_b[:, q * 512:(q + 1) * 512], start=False, stop=False)
                        last.then_inc(s_lora, 1)
                    if more and t in TURN:
                        if t == 4:
                            pe.wait_ge(s_x[1 - w], 16 * (v + 1 + w))
                        for j in TURN[t]:
                            transpose_slot(pp + 1, 1 - w, j)

            for h in range(HALVES):
                last_h = h + 1 == HALVES
                with pe.Fori(0, NB - last_h) as b:
                    pair_products(h, b, 0, True)
                    pair_products(h, b, 1, True)
                if last_h:
                    pair_products(h, NB - 1, 0, True)
                    pair_products(h, NB - 1, 1, False)


_INS = ['x', 'itok_B_1_7', 'L0_cond_weight', 'L0_cond_bias', 'L0_cond_lora_a_weights', 'L0_cond_lora_b_weights',
        'L0_cond_scaling_factors', 'L0_ffn_codes', 'L0_ffn_absmax', 'L0_ffn_bias']


def kernel(**inputs):
    import concourse.bacc as _bacc
    from concourse.bass_utils import run_bass_kernel_spmd as _run

    nc = _bacc.Bacc("TRN2", target_bir_lowering=False, num_devices=1)
    arrays, args = {}, []
    rows = np.arange(128)
    rank = inputs['L0_cond_lora_a_weights'].shape[1]
    consts = {
        'identity': np.eye(128, dtype=np.float32),
        'rank_of': (rows[:, None] % rank == np.arange(rank)[None, :]).astype(np.float32),
        'adapter_of': (rows[:, None] // rank).astype(np.float32),
        'restack': (np.arange(2 * rank)[:, None] % rank == np.arange(3 * rank)[None, :] % rank).astype(np.float32),
    }
    for name in _INS + list(consts):
        a = np.ascontiguousarray(inputs[name] if name in _INS else consts[name])
        arrays[f"in_{name}_dram"] = a
        args.append(nc.dram_tensor(f"in_{name}_dram", a.shape, mybir.dt.from_np(a.dtype), kind="ExternalInput").ap())
    shape = tuple(inputs['x'].shape)
    args.append(nc.dram_tensor("out_0_dram", shape, mybir.dt.float32, kind="ExternalOutput").ap())
    adaln_ffn_kernel(nc, *args)
    r = _run(nc, [arrays], core_ids=[0])
    return r.results[0]["out_0_dram"]
```

```python
import numpy as np
import concourse.bass as bass
from concourse import mybir
from contextlib import ExitStack


def adaln_ffn_kernel(
    nc: bass.Bass,
    x: bass.AP,
    itok: bass.AP,
    weight: bass.AP,
    bias1: bass.AP,
    lora_a: bass.AP,
    lora_b: bass.AP,
    scaling: bass.AP,
    codes: bass.AP,
    absmax: bass.AP,
    bias2: bass.AP,
    identity: bass.AP,
    rank_of: bass.AP,
    adapter_of: bass.AP,
    restack: bass.AP,
    out: bass.AP,
):
    F32, F32R = mybir.dt.float32, mybir.dt.float32r
    I32, I16, BF16 = mybir.dt.int32, mybir.dt.int16, mybir.dt.bfloat16
    ALU, ACT = mybir.AluOpType, mybir.ActivationFunctionType
    P = 128
    NB, S, D = x.shape
    KT = D // P
    NA, R = lora_a.shape[0], lora_a.shape[1]
    QBLOCK = 64
    NQ = D // QBLOCK
    HI, LO = 0, 1

    NF4 = [-1.0, -0.6961928009986877, -0.5250730514526367, -0.39491748809814453, -0.28444138169288635,
           -0.18477343022823334, -0.09105003625154495, 0.0, 0.07958029955625534, 0.16093020141124725,
           0.24611230194568634, 0.33791524171829224, 0.44070982933044434, 0.5626170039176941,
           0.7229568362236023, 1.0]
    ZERO_CODE = 7
    STEP = 14
    LADDER = STEP << 7

    def rung(k):
        return float(np.float32(NF4[k])) * 2.0 ** (127 - STEP * abs(k - ZERO_CODE))

    CHUNKS = [256, 256, 384, 384, 384, 384]
    assert sum(CHUNKS) == D and CHUNKS[0] == 2 * P
    NCH = len(CHUNKS)
    LAST = NCH - 1
    O0 = [D - sum(CHUNKS[:c + 1]) for c in range(NCH)]
    OT = [n // P for n in CHUNKS]
    WQ_COLS = max(CHUNKS)
    QD = 512
    NJ = D // QD
    UT = KT // NJ
    DT = QD // P
    PIECE0 = [NJ * sum(OT[:c]) for c in range(NCH + 1)]
    TILES = KT + 1
    G = TILES * NCH
    STEPS = KT + 2
    BUF0 = [[NJ * sum(1 for cc in range(c) if OT[cc] > u) for u in range(3)] for c in range(NCH + 1)]
    DEQ_OPS = 13
    BLOCKS = 2 * NJ
    NST = 4

    HALVES, HO = 2, D // 2
    COL = [D - (h + 1) * HO for h in range(HALVES)]
    NO = HO // 512
    ACC = 2 * NO
    PT = 256
    PAIRS = NB * S // PT
    K_LORA = 3 * R + 4
    TURN = {t: ([2 * (t - 4), 2 * (t - 4) + 1] if t < 8 else [t]) for t in range(4, KT)}
    LOW_STEPS = range(1, 1 + KT // 2)
    RESTACK_STEP, LORA_STEP = 11, 14
    PLACE = [8, 9, 10, 11, 0, 1, 2, 3, 4, 5, 12, 13, 14, 15, 6, 7]
    XG = 2
    LOADED = KT // XG
    MAKE, LOAD = "make", "load"
    FIRST_SLOTS = {KT - 4: [0, 1, 2], KT - 3: [3, 4, 5], KT - 2: [6, 7, 8], KT - 1: [9, 10, 11],
                   KT: [12, 13, 14], KT + 1: [15]}

    b_cols = nc.dram_tensor("b_cols", [D, NA * R], F32).ap()
    wt_d = nc.dram_tensor("wt_d", [KT, P, D], F32).ap()
    a_sel_d = nc.dram_tensor("a_sel_d", [NB, P, KT * 2 * R], F32).ap()
    g_d = [nc.dram_tensor(f"g_d{i}", [NB * R, D], F32).ap() for i in range(2)]
    bt_d = [nc.dram_tensor(f"bt_d{i}", [2, D], F32).ap() for i in range(2)]
    xt_d = nc.dram_tensor("xt_d", [P, PAIRS, KT, PT], F32).ap()
    low_d = nc.dram_tensor("low_d", [PAIRS, K_LORA, PT], F32).ap()

    ctx = ExitStack()
    with ctx:
        sem = lambda name: ctx.enter_context(nc.semaphore(name))
        base = (nc.sbuf_base + 31) // 32 * 32
        KB = 1024

        def at(name, kb, shape, dt):
            return nc.alloc_sbuf_tensor_at(name, shape, dt, offset=base + int(kb * KB))

        wq_t = [at(f"wq_t{i}", 48 * i, [P, 2, KT, WQ_COLS], F32R) for i in range(2)]
        v_sb = at("v_sb", 96, [P, WQ_COLS], F32)
        bt_sb = at("bt_sb", 97.5, [2, WQ_COLS], F32)
        bias2_sb = at("bias2_sb", 99, [1, WQ_COLS], F32)
        g_hl = [at(f"g_hl{i}", 100.5 + 1.5 * i, [P, WQ_COLS], F32) for i in range(2)]
        bt_hl = [at(f"bt_hl{i}", 103.5 + 1.5 * i, [2, WQ_COLS], F32) for i in range(2)]
        code_t = [at(f"code_t{i}", 112 + 2 * i, [P, QD], I32) for i in range(3)]
        ladder = [at(f"ladder{i}", 118 + 2 * i, [P, 2, QD], I16) for i in range(3)]
        w_nat = [at(f"w_nat{i}", 128 + 8 * i, [P, KT, P], F32) for i in range(2)]
        w_hl = [at(f"w_hl{i}", 144 + 16 * i, [P, 2, KT, P], F32R) for i in range(2)]
        deq = [at(f"deq{i}", 176 + 2 * i, [P, QD], F32) for i in range(4)]
        wq_nat = [at(f"wq_nat{i}", 184 + 2 * i, [P, QD], F32) for i in range(3)]
        wt_st = [at(f"wt_st{i}", 192 + 1.5 * i, [P, WQ_COLS], F32) for i in range(NST)]
        absm = at("absm", 190, [P, D // P, NQ], F32)
        sel = at("sel", 198, [P, NB, R], F32)
        sel_s = at("sel_s", 198.5, [P, NB, R], F32)
        b1_nat = at("b1_nat", 199, [P, KT], F32)
        b1_hl = at("b1_hl", 199.0625, [P, KT, 2], F32R)
        rank_c = at("rank_c", 199.25, [P, R], F32)
        adapt_c = at("adapt_c", 199.3125, [P, 1], F32)
        scale_c = at("scale_c", 199.34375, [P, 1], F32)
        ids_i = at("ids_i", 199.375, [P, NB], I32)
        ids_f = at("ids_f", 199.40625, [P, NB], F32)
        ids_w = at("ids_w", 199.4375, [P, NB], F32)
        hit = at("hit", 199.46875, [P, NB], F32)
        bias_l = at("bias_l", 199.5, [P, 1], F32)
        warm = at("warm", 199.5625, [P, 1], F32)
        bias_h = at("bias_h", 199.53125, [P, 1], F32)
        a_nat = at("a_nat", 40, [P, D], F32)
        a_sel = at("a_sel", 24, [P, NB, KT, 2, R], F32)
        x_nat = [at(f"x_nat{i}", 176 * i, [P, 2, D], F32) for i in range(2)]
        x_t = at("x_t", 16, [P, KT, 2, PT], F32R)
        wt = at("wt", 48, [P, KT, 2, HO], F32R)
        a_b = at("a_b", 200, [P, KT, 2 * R], F32R)
        g_b = at("g_b", 196, [K_LORA, HO], F32R)
        low_sb = at("low_sb", 202, [2 * R, PT], F32)
        low_st = at("low_st", 203, [K_LORA, PT], F32R)
        x_st = [at(f"x_st{i}", 204 + i, [P, PT], F32) for i in range(2)]
        ident = at("ident", 206, [P, P], F32)
        rst = at("rst", 206.5, [2 * R, 3 * R], F32)

        ps = [ctx.enter_context(nc.psum_tensor(f"ps{i}", [P, 512], F32)) for i in range(8)]
        acc1, tr1, a_ps, g_ps = ps[0:2], ps[2:5], ps[2:6], ps[7]
        block_ps = [ps[0], ps[1], ps[6], ps[7]]
        tr_first = ps[4:7]
        acc2, rst_ps, tr2, low_ps = ps[0:4], ps[4], ps[5:7], ps[7]

        s_const = sem("const_loaded")
        s_small = sem("small_loaded")
        s_a_nat = sem("a_nat_loaded")
        s_bcols = sem("b_cols_stored")
        s_sel = sem("sel_chain")
        s_a_mm = sem("a_selected")
        s_a_hi = sem("a_hi_done")
        s_a_lo = sem("a_lo_done")
        s_a_st = sem("a_sel_stored")
        s_b1hi = sem("b1_hi_done")
        s_b1 = sem("b1_split")
        s_absm = sem("absmax_loaded")
        s_code = [sem(f"codes_loaded{i}") for i in range(3)]
        s_ladder = sem("ladder_made")
        s_dq = sem("dequantise_chain")
        s_piece = sem("piece_dequantised")
        s_tr1 = sem("piece_transposed")
        s_qhi = sem("wq_hi_done")
        s_qlo = sem("wq_lo_done")
        s_w = [sem(f"w_loaded{i}") for i in range(2)]
        s_whi = sem("w_hi_done")
        s_wlo = sem("w_lo_done")
        s_mm1 = sem("w_tile_multiplied")
        s_evac1 = sem("acc1_evacuated")
        s_wtst = [sem(f"wt_stored{i}") for i in range(NST)]
        s_bias2 = sem("bias2_loaded")
        s_gmm = sem("v_selected")
        s_btadd = sem("bt_added")
        s_ghi = sem("g_hi_done")
        s_bthi = sem("bt_hi_done")
        s_glo = sem("g_lo_done")
        s_gst = sem("g_stored")
        s_wt = [sem(f"wt_loaded{t}") for t in range(KT)]
        s_wthi = sem("wt_hi_done")
        s_wtlo = sem("wt_lo_done")
        s_xa = [sem(f"x_lower_loaded{i}") for i in range(2)]
        s_xb = [sem(f"x_upper_loaded{i}") for i in range(2)]
        s_ab = sem("a_b_loaded")
        s_gb = sem("g_b_loaded")
        s_tr2 = sem("x_transposed")
        s_xraw = sem("x_staged")
        s_xst = [sem(f"x_stored{i}") for i in range(2)]
        s_xld = [sem(f"x_t_loaded{g}") for g in range(KT // 2)]
        s_xhi = sem("x_hi_done")
        s_xlo = sem("x_lo_done")
        s_step = sem("steps_done")
        s_low = sem("low_done")
        s_lowev = sem("low_evacuated")
        s_rst = sem("low_restacked")
        s_lsthi = sem("low_stack_hi")
        s_lstone = sem("low_stack_ones")
        s_lst = sem("low_stack_done")
        s_lowst = sem("low_stored")
        s_lowld = sem("low_loaded")
        s_lora = sem("lora_added")
        s_acc = sem("acc2_done")
        s_evac2 = sem("acc2_evacuated")
        s_out = [sem(f"out_stored{i}") for i in range(2)]

        block = ctx.enter_context(nc.Block())

        def piece_at(c, j, u, ahead):
            u += ahead
            while c < NCH and u >= OT[c]:
                u -= OT[c]
                if isinstance(j, int) and j == NJ - 1:
                    c, j = c + 1, 0
                else:
                    j = j + 1
            return (c, j, u) if c < NCH else None

        def number(c, j, u):
            return PIECE0[c] + u + j * OT[c]

        def wqt_part(c, hl, j, u):
            t = wq_t[c % 2]
            return t[:, hl, bass.ds(j * DT, DT), u * P:(u + 1) * P]

        def groups(eng, c, step, select_a):
            first = BLOCKS // UT if c == 0 else 0
            with eng.Fori(first, NJ - 1) as j:
                for u in range(UT):
                    step(j, u)
            if c == LAST:
                select_a()
            for u in range(UT):
                step(NJ - 1, u)

        def piece_of_step(c, j, u):
            if c == 0:
                return (1, 2 * j - NJ + u // 2, u % 2)
            return (c + 1, j, u) if c + 1 < NCH and u < OT[c + 1] else None

        @block.sync
        def _(sp):
            def load_codes(c, j, u):
                sp.wait_ge(s_ladder, number(c, j, u) + 1)
                row = O0[c] + u * P
                sp.dma_start(code_t[u][:, :], codes[row:row + P, bass.ds(j * QD, QD)]).then_inc(s_code[u], 16)

            def load_tile(c, s_static, s, src):
                g0 = TILES * c + s_static
                g = TILES * c + s
                sp.wait_ge(s_wlo, 2 * g + 2)
                dst = w_nat[g0 % 2][:, :, :]
                if src.shape[1] != KT:
                    dst = dst.rearrange("p k i -> p (k i)").rearrange("p (t i) -> p t i", t=src.shape[1])
                sp.dma_start(dst, src).then_inc(s_w[g0 % 2], 16)

            def w_src(s):
                return weight.rearrange("(t p) i -> p t i", p=P)[:, :, bass.ds(s * P, P)]

            def block_src(s):
                q, half = divmod(s, 2)
                return weight.rearrange("(t p) i -> p t i", p=P)[:, q * DT:(q + 1) * DT,
                                                                 half * UT * P:(half + 1) * UT * P]

            b_src = b_cols.rearrange("(t p) r -> p t r", p=P)

            def store_wt(c, u, s):
                sp.wait_ge(s_evac1, 2 + STEPS * c + s + 1)
                n = CHUNKS[c]
                dst = wt_d.rearrange("k p o -> p k o")[:, bass.ds(s, 1), O0[c]:O0[c] + n].rearrange(
                    "p k o -> p (k o)")
                sp.dma_start(dst, wt_st[u % NST][:, 0:n]).then_inc(s_wtst[u % NST], 16)

            def store_g(c):
                sp.wait_ge(s_ghi, c + 1)
                sp.wait_ge(s_bthi, c + 1)
                sp.wait_ge(s_glo, 2 * (c + 1))
                cols = slice(O0[c], O0[c] + CHUNKS[c])
                for hl in (HI, LO):
                    sp.dma_start(g_d[hl][:, cols], g_hl[hl][:, 0:CHUNKS[c]]).then_inc(s_gst, 16)
                    sp.dma_start(bt_d[hl][:, cols], bt_hl[hl][:, 0:CHUNKS[c]]).then_inc(s_gst, 16)

            def store_slot(pp, j):
                sp.wait_ge(s_xraw, pp * KT + j + 1)
                dst = xt_d[:, bass.ds(pp, 1), j, :].rearrange("p n t -> p (n t)")
                sp.dma_start(dst, x_st[j % 2][:, :]).then_inc(s_xst[j % 2], 16)

            x_p = x.rearrange("b (q u p) d -> p (b q) u d", u=2, p=P)
            o_p = out.rearrange("b (q u p) d -> p (b q) u d", u=2, p=P)

            def load_a(b):
                src = a_sel_d.rearrange("b p f -> p b f")[:, bass.ds(b, 1), :].rearrange("p b f -> p (b f)")
                sp.dma_start(a_b[:, :, :].rearrange("p k r -> p (k r)").bitcast(F32), src).then_inc(s_ab, 16)

            def load_g(h, b):
                cols = slice(COL[h], COL[h] + HO)
                for row, hl in ((0, HI), (R, LO), (2 * R, HI)):
                    sp.dma_start(g_b[row:row + R, :].bitcast(F32), g_d[hl][bass.ds(b * R, R), cols]
                                 ).then_inc(s_gb, 16)
                for hl in (HI, LO):
                    row = 3 * R + 2 * hl
                    sp.dma_start(g_b[row:row + 2, :].bitcast(F32), bt_d[hl][:, cols]).then_inc(s_gb, 16)

            def load_x(par, pp, upper):
                cols = slice(HO, D) if upper else slice(0, HO)
                src = x_p[:, bass.ds(pp, 1), :, cols].rearrange("p n u d -> p (n u) d")
                sp.dma_start(x_nat[par][:, :, cols], src).then_inc((s_xb if upper else s_xa)[par], 16)

            for q in s_wtst + s_xst + [s_lowst]:
                sp.sem_inc(q, 16)
            load_codes(0, 0, 0)
            load_codes(0, 0, 1)
            sp.dma_start(absm[:, :, :], absmax.rearrange("(t p b) -> p t b", p=P, b=NQ)).then_inc(s_absm, 16)
            load_tile(0, 0, 0, block_src(0))
            load_codes(*piece_at(0, 0, 0, 2))
            load_tile(0, 1, 1, block_src(1))
            sp.dma_start(ids_i[:, :], itok.partition_broadcast(P)).then_inc(s_small, 16)
            sp.dma_start(scale_c[:, :], bass.AP(scaling.tensor, scaling.offset, [[1, NA], [0, R], [1, 1]])
                         ).then_inc(s_small, 16)
            sp.dma_start(b1_nat[:, :], bias1.rearrange("(t p) -> p t", p=P),
                         allow_slow_non_contiguous=True).then_inc(s_small, 16)
            sp.dma_start(rank_c[:, :], rank_of).then_inc(s_const, 16)
            sp.dma_start(adapt_c[:, :], adapter_of).then_inc(s_const, 16)
            sp.dma_start(ident[:, :], identity).then_inc(s_const, 16)
            sp.dma_start(rst[:, :], restack).then_inc(s_const, 16)

            for s in range(BLOCKS):
                if s >= 2:
                    load_tile(0, s, s, block_src(s))
                if s:
                    load_codes(*piece_at(0, s // OT[0], s % OT[0], 2))
                if s == 3:
                    for a in range(NA):
                        sp.dma_start(b_cols[:, a * R:(a + 1) * R], lora_b[a]).then_inc(s_bcols, 16)

            def codes_of(c, j, u):
                piece = piece_of_step(c, j, u)
                nxt = piece and piece_at(*piece, 2)
                if nxt:
                    load_codes(*nxt)

            for c in range(NCH):
                def step(j, u):
                    s = j * UT + u
                    static = isinstance(j, int)
                    load_tile(c, u, s, w_src(s))
                    if u:
                        codes_of(c, j, u - 1)
                    elif c == 0 and j == NJ - 1:
                        codes_of(c, j - 1, UT - 1)
                    if static and s == 1 and c:
                        store_wt(c - 1, KT - 1, KT - 1)
                    if static and s == 2 and c:
                        store_g(c - 1)
                    if static and s == 2 and c == LAST:
                        sp.wait_ge(s_mm1, STEPS * c)
                        sp.dma_start(a_nat[:, :], lora_a.rearrange("a r i -> (a r) i")).then_inc(s_a_nat, 16)
                    if static and c == LAST and s in (3, KT - UT):
                        load_x(0, 0, s > 3)
                    if static and c == LAST and s in (KT - UT + 1, KT - UT + 2):
                        sp.wait_ge(s_tr1, 2 + PIECE0[NCH])
                        load_x(1, 1, s > KT - UT + 1)
                    if not static or s >= 3:
                        if c == 0 and static and s < BLOCKS + 4:
                            ready = {BLOCKS: [], BLOCKS + 1: range(0, UT), BLOCKS + 2: [],
                                     BLOCKS + 3: range(UT, BLOCKS + 1)}[s]
                            for r in ready:
                                store_wt(0, r, r)
                        else:
                            store_wt(c, u + 1, s - 3)
                    if c == LAST and static and s == KT - 2:
                        sp.wait_ge(s_a_hi, 4)
                        sp.wait_ge(s_a_lo, 4)
                        sp.dma_start(a_sel_d.rearrange("b p f -> p b f"),
                                     a_sel[:, :, :, :, :].rearrange("p b k h r -> p b (k h r)")).then_inc(s_a_st, 16)
                    if c == LAST and static and s >= KT - 1:
                        for t in range(KT - 4, s - 2):
                            for i in FIRST_SLOTS[t]:
                                store_slot(0, i)

                first = BLOCKS // UT if c == 0 else 0
                for u in range(UT):
                    step(first, u)
                if first + 1 < NJ - 1:
                    with sp.Fori(first + 1, NJ - 1) as j:
                        for u in range(UT):
                            step(j, u)
                for u in range(UT):
                    step(NJ - 1, u)
                codes_of(c, NJ - 1, UT - 1)
                if c == LAST:
                    sp.wait_ge(s_a_st, 16)
                    load_a(0)
                if c == 0:
                    sp.wait_ge(s_bcols, 16 * NA)
                load_tile(c, KT, KT, b_src)
                if c:
                    sp.wait_ge(s_btadd, c)
                sp.dma_start(bias2_sb[:, 0:CHUNKS[c]], bias2[O0[c]:O0[c] + CHUNKS[c]].rearrange(
                    "(a o) -> a o", a=1)).then_inc(s_bias2, 16)
                store_wt(c, KT - 3, KT - 3)
                if c == LAST:
                    for i in FIRST_SLOTS[KT - 3]:
                        store_slot(0, i)
                store_wt(c, KT - 2, KT - 2)
                if c == LAST:
                    for i in FIRST_SLOTS[KT - 2]:
                        store_slot(0, i)
                    store_wt(c, KT - 1, KT - 1)
                    for t in (KT - 1, KT, KT + 1):
                        for i in FIRST_SLOTS[t]:
                            store_slot(0, i)
                if c == LAST:
                    for q in s_wtst:
                        sp.wait_ge(q, 16 * (1 + NJ * NCH))
                    sp.wait_ge(s_gmm, NCH)
                    sp.wait_ge(s_gst, 4 * 16 * LAST)
                    load_g(0, 0)
                    store_g(LAST)

            def load_slots(pp, g):
                dst = x_t[:, g * XG:(g + 1) * XG, LO, :].bitcast(F32)
                src = xt_d[:, bass.ds(pp - PAIRS, 1), g * XG:(g + 1) * XG, :]
                sp.dma_start(dst, src.rearrange("p n k t -> p (n k) t")).then_inc(s_xld[g], 16)

            def low_of(pp):
                return low_d.rearrange("n k t -> k n t")[:, bass.ds(pp, 1), :].rearrange("k n t -> k (n t)")

            def store_pair(h, b, w):
                pp = (h * NB + b) * 2 + w
                for u in range(2):
                    sp.wait_ge(s_evac2, ACC * (pp + 1) + NO * (u + 1))
                    dst = o_p[:, bass.ds(2 * b + w, 1), u, COL[h]:COL[h] + HO].rearrange("p n d -> p (n d)")
                    sp.dma_start(dst, x_nat[w][:, u, COL[h]:COL[h] + HO]).then_inc(s_out[w], 16)

            def traffic(h, b, w, mode, following, first=False):
                v = h * NB + b
                pp = 2 * v + w
                o = 1 - w
                if not first and mode == (LOAD if h else MAKE):
                    sp.wait_ge(s_out[o], 16 * 2 * (v + w))
                    load_x(o, pp + 1 - h * PAIRS, h == 0)
                if h == 0 and following:
                    sp.wait_ge(s_tr2, KT * (pp + 1))
                    load_x(w, pp + 2 if following[0] == 0 else w, False)
                if mode == MAKE:
                    for t in range(KT - 1):
                        for j in TURN.get(t, ()):
                            store_slot(pp + 1, j)
                if mode == LOAD:
                    for g in range(LOADED - 1):
                        sp.wait_ge(s_step, (KT - 1) * pp + max(XG * (g + 1), 3))
                        load_slots(pp + 1, g)
                if h == 0:
                    sp.wait_ge(s_lst, pp + 1)
                    sp.dma_start(low_of(pp), low_st[:, :].bitcast(F32)).then_inc(s_lowst, 16)
                    if w == 1 and following and following[0] == 0:
                        sp.wait_ge(s_low, pp + 1)
                        load_a(following[1])
                if w == 1 and following:
                    sp.wait_ge(s_lora, pp + 1)
                    load_g(*following)
                if mode == LOAD:
                    if h == 0:
                        sp.wait_ge(s_lowst, 16 * (1 + PAIRS))
                    sp.wait_ge(s_lora, pp + 1)
                    sp.dma_start(low_st[:, :].bitcast(F32), low_of(pp + 1 - PAIRS)).then_inc(s_lowld, 16)
                store_pair(h, b, w)
                if mode == MAKE:
                    store_slot(pp + 1, KT - 1)
                if mode == LOAD:
                    sp.wait_ge(s_acc, 2 * NO * (pp + 1))
                    load_slots(pp + 1, LOADED - 1)

            traffic(0, 0, 0, MAKE, (0, 1), first=True)
            traffic(0, 0, 1, MAKE, (0, 1))
            with sp.Fori(1, NB - 1) as b:
                for w in range(2):
                    traffic(0, b, w, MAKE, (0, b + 1))
            traffic(0, NB - 1, 0, MAKE, (1, 0))
            for q in s_xst:
                sp.wait_ge(q, 16 * (1 + PAIRS * KT // 2))
            traffic(0, NB - 1, 1, LOAD, (1, 0))
            traffic(1, 0, 0, LOAD, (1, 1), first=True)
            traffic(1, 0, 1, LOAD, (1, 1))
            with sp.Fori(1, NB - 1) as b:
                for w in range(2):
                    traffic(1, b, w, LOAD, (1, b + 1))
            traffic(1, NB - 1, 0, LOAD, None)
            traffic(1, NB - 1, 1, None, None)
            for q in s_out:
                sp.wait_ge(q, 16 * 2 * HALVES * NB)

        @block.gpsimd
        def _(pool):
            def split_lo(c, u, s, half):
                g0, g = TILES * c + u, TILES * c + s
                par, rows = g0 % 2, slice(half * KT // 2, (half + 1) * KT // 2)
                pool.wait_ge(s_whi, 2 * g + half + 1)
                nc.gpsimd.tensor_tensor(w_hl[par][:, LO, rows, :], w_nat[par][:, rows, :],
                                        w_hl[par][:, HI, rows, :].bitcast(F32), ALU.subtract).then_inc(s_wlo, 1)

            pool.sem_inc(s_wlo, 4)
            for c in range(NCH):
                with pool.Fori(0, NJ) as j:
                    for u in range(UT):
                        for half in range(2):
                            split_lo(c, u, j * UT + u, half)
                for half in range(2):
                    split_lo(c, KT, KT, half)

            for h in range(HALVES):
                for t in range(KT):
                    place = PLACE[t]
                    pool.wait_ge(s_wthi, h * KT + t + 1)
                    nc.gpsimd.tensor_tensor(wt[:, place, LO, :], wt[:, place, LO, :].bitcast(F32),
                                            wt[:, place, HI, :].bitcast(F32), ALU.subtract).then_inc(s_wtlo, 1)

        @block.scalar
        def _(act):
            def make_ladders(c, j, u):
                cnt = BUF0[c][u] + j
                act.wait_ge(s_code[u], 16 * (cnt + 1))
                act.wait_ge(s_piece, number(c, j, u) + 1)
                nc.scalar.activation(ladder[u][:, 0, :], code_t[u][:, :], ACT.Relu, bias=bias_l[:, 0:1],
                                     scale=float(LADDER))
                nc.scalar.activation(ladder[u][:, 1, :], code_t[u][:, :], ACT.Relu, bias=bias_h[:, 0:1],
                                     scale=-float(LADDER)).then_inc(s_ladder, 1)

            def piece_hi(c, j, u):
                act.wait_ge(s_tr1, 2 + number(c, j, u) + 1)
                nc.scalar.copy(wqt_part(c, HI, j, u), tr1[u][:, :].rearrange("p (t o) -> p t o", t=DT)
                               ).then_inc(s_qhi, 1)

            def split_hi(g0, g, between=lambda: None):
                par = g0 % 2
                act.wait_ge(s_w[par], 16 * (g0 // 2 + 1) + 8 * (g - g0))
                for half in range(2):
                    rows = slice(half * KT // 2, (half + 1) * KT // 2)
                    nc.scalar.copy(w_hl[par][:, HI, rows, :], w_nat[par][:, rows, :]).then_inc(s_whi, 1)
                    if half == 0:
                        between()

            def evacuate(c, u, j, src):
                act.wait_ge(s_wtst[u], 16 * (1 + NJ * c + j))
                nc.scalar.copy(wt_st[u][:, 0:CHUNKS[c]], src).then_inc(s_evac1, 1)

            def load_wt(h, t):
                act.dma_start(wt[:, PLACE[t], LO, :].bitcast(F32), wt_d[t, :, COL[h]:COL[h] + HO]
                              ).then_inc(s_wt[t], 16)

            def wt_hi(h, t):
                act.wait_ge(s_wt[t], 16 * (h + 1))
                nc.scalar.copy(wt[:, PLACE[t], HI, :], wt[:, PLACE[t], LO, :].bitcast(F32)).then_inc(s_wthi, 1)

            def stage_and_hi(j, bank):
                nc.scalar.copy(x_st[j % 2][:, :], bank[:, 0:PT]).then_inc(s_xraw, 1)
                nc.scalar.copy(x_t[:, j, HI, :], bank[:, 0:PT]).then_inc(s_xhi, 1)

            def first_hi(t):
                if t == KT - 3:
                    act.wait_ge(s_a_st, 16)
                for j in FIRST_SLOTS.get(t, ()):
                    act.wait_ge(s_tr2, j + 1)
                    act.wait_ge(s_xst[j % 2], 16 * (1 + j // 2))
                    stage_and_hi(j, tr_first[j % 3])

            act.wait_ge(s_sel, 2)
            nc.scalar.activation(warm[:, :], bias_l[:, :], ACT.Relu)
            make_ladders(0, 0, 0)
            make_ladders(0, 0, 1)
            split_hi(0, 0)
            split_hi(1, 1)
            act.wait_ge(s_small, 48)
            nc.scalar.copy(b1_hl[:, :, HI], b1_nat[:, :]).then_inc(s_b1hi, 1)

            def piece_ladders(c, j, u):
                nxt = piece_at(c, j, u, 2)
                if nxt:
                    make_ladders(*nxt)

            def piece_step(c, j, u):
                piece_ladders(c, j, u)
                piece_hi(c, j, u)

            def select_a():
                for q in range(4):
                    act.wait_ge(s_a_mm, q + 1)
                    dst = a_sel[:, :, q * 4:(q + 1) * 4, HI, :].bitcast(F32R).rearrange("p b k r -> p k b r")
                    nc.scalar.copy(dst, a_ps[q][:, :].rearrange("p (k b r) -> p k b r", k=4, b=NB)
                                   ).then_inc(s_a_hi, 1)

            n = CHUNKS[0]
            for u in range(OT[0]):
                piece_step(0, 0, u)
            for q in range(NJ):
                for half in range(2):
                    act.wait_ge(s_mm1, 2 * q + half + 1)
                    split_hi(2 * q + half + 2, 2 * q + half + 2,
                             lambda: q + 1 < NJ and piece_hi(0, q + 1, half))
                    if q == NJ - 1:
                        for u in range(UT):
                            i = half * UT + u
                            evacuate(0, u, half, block_ps[i // 2][:, i % 2 * n:(i % 2 + 1) * n])
                    else:
                        piece_ladders(0, q + 1, half)
            for c in range(NCH):
                n = CHUNKS[c]
                if c == LAST:
                    act.wait_ge(s_piece, 2 + PIECE0[NCH])
                    for q in s_wtst:
                        act.wait_ge(q, 16 * (1 + NJ * (NCH - 2)))
                    load_wt(0, 0)
                    load_wt(0, 1)

                def step(j, u):
                    s = j * UT + u
                    g0, g = TILES * c + u, TILES * c + s
                    act.wait_ge(s_mm1, STEPS * c + s + 1)
                    piece = piece_of_step(c, j, u)
                    if not (isinstance(s, int) and g + 2 >= G):
                        split_hi(g0 + 2, g + 2, lambda: piece and piece_hi(*piece))
                    if piece:
                        piece_ladders(*piece)
                    evacuate(c, u, j, acc1[u % 2][:, 0:n])
                    if c == LAST and isinstance(s, int):
                        first_hi(s)

                groups(act, c, step, select_a)
                if c == LAST:
                    act.wait_ge(s_wlo, 4 + 2 * G)
                    load_wt(0, 2)
                    load_wt(0, 3)
                    wt_hi(0, 0)
                    wt_hi(0, 1)
                act.wait_ge(s_mm1, STEPS * c + KT + 1)
                if c < LAST:
                    split_hi(TILES * c + KT + 2, TILES * c + KT + 2)
                if c:
                    act.wait_ge(s_gmm, c)
                nc.scalar.copy(v_sb[:, 0:n], acc1[0][:, 0:n]).then_inc(s_evac1, 1)
                if c == LAST:
                    first_hi(KT)
                    wt_hi(0, 2)
                act.wait_ge(s_mm1, STEPS * c + KT + 2)
                if c:
                    act.wait_ge(s_glo, 2 * c)
                nc.scalar.copy(bt_sb[:, 0:n], acc1[1][0:2, 0:n]).then_inc(s_evac1, 1)
                if c == LAST:
                    for t in range(4, KT - 2):
                        load_wt(0, t)
                    first_hi(KT + 1)
                if c:
                    act.wait_ge(s_gst, 4 * 16 * c)
                act.wait_ge(s_btadd, c + 1)
                nc.scalar.copy(bt_hl[HI][:, 0:n].bitcast(F32R), bt_sb[:, 0:n]).then_inc(s_bthi, 1)
                act.wait_ge(s_gmm, c + 1)
                nc.scalar.copy(g_hl[HI][:, 0:n].bitcast(F32R), g_ps[:, 0:n]).then_inc(s_ghi, 1)

            def slot_hi(pp, j):
                act.wait_ge(s_tr2, pp * KT + j + 1)
                act.wait_ge(s_xst[j % 2], 16 * (1 + pp * KT // 2 + j // 2))
                stage_and_hi(j, tr2[j % 2])

            def loaded_hi(pp, j):
                act.wait_ge(s_xld[j // XG], 16 * (pp - PAIRS + 1))
                nc.scalar.copy(x_t[:, j, HI, :], x_t[:, j, LO, :].bitcast(F32)).then_inc(s_xhi, 1)

            def pair_hi(pp, h, mode, weights=None):
                if h:
                    for j in range(KT):
                        loaded_hi(pp + 1, j)
                    return
                for t in range(KT):
                    if weights == "rest":
                        if t == 9:
                            act.wait_ge(s_gst, 4 * 16 * NCH)
                            load_wt(0, KT - 2)
                            load_wt(0, KT - 1)
                        if t + 3 < KT:
                            wt_hi(0, t + 3)
                    if weights == "next" and t:
                        act.wait_ge(s_step, (KT - 1) * pp + t)
                        load_wt(1, t - 1)
                        if t >= 4:
                            wt_hi(1, t - 4)
                    if t == LOW_STEPS[-1]:
                        act.wait_ge(s_low, pp + 1)
                        nc.scalar.copy(low_sb[:, :], low_ps[0:2 * R, 0:PT]).then_inc(s_lowev, 1)
                    if t == RESTACK_STEP:
                        act.wait_ge(s_rst, pp + 1)
                        act.wait_ge(s_lowst, 16 * (pp + 1))
                        nc.scalar.copy(low_st[0:3 * R, :], rst_ps[0:3 * R, 0:PT]).then_inc(s_lsthi, 1)
                    if mode == MAKE:
                        for j in TURN.get(t, ()):
                            slot_hi(pp + 1, j)
                    if mode == LOAD and t >= 3:
                        loaded_hi(pp + 1, t - 3)
                if weights == "next":
                    act.wait_ge(s_acc, ACC * (pp + 1))
                    load_wt(1, KT - 1)
                    for t in range(KT - 4, KT):
                        wt_hi(1, t)
                if mode == LOAD:
                    for j in range(KT - 3, KT):
                        loaded_hi(pp + 1, j)

            act.wait_ge(s_lstone, 1)
            pair_hi(0, 0, MAKE, "rest")
            pair_hi(1, 0, MAKE)
            with act.Fori(1, NB - 1) as b:
                for w in range(2):
                    pair_hi(2 * b + w, 0, MAKE)
            pair_hi(PAIRS - 2, 0, MAKE)
            pair_hi(PAIRS - 1, 0, LOAD, "next")
            with act.Fori(NB, 2 * NB - 1) as v:
                for w in range(2):
                    pair_hi(2 * v + w, 1, LOAD)
            pair_hi(HALVES * PAIRS - 2, 1, LOAD)

        @block.vector
        def _(dve):
            count = [0]

            def link(ins):
                count[0] += 1
                ins.then_inc(s_sel, 1)
                dve.wait_ge(s_sel, count[0])

            dve.sem_inc(s_ladder, 2)
            dve.sem_inc(s_piece, 2)
            dve.sem_inc(s_tr1, 2)
            dve.sem_inc(s_qlo, 2)
            dve.sem_inc(s_evac1, 2)
            dve.sem_inc(s_xlo, 2)
            dve.sem_inc(s_evac2, ACC)
            nc.vector.memset(low_st[:, :].bitcast(F32), 1.0).then_inc(s_lstone, 1)
            link(nc.vector.memset(bias_l[:, :], -float(ZERO_CODE * LADDER)))
            link(nc.vector.memset(bias_h[:, :], float(ZERO_CODE * LADDER)))
            def dequantise(c, j, u, between=lambda: None, early=False):
                n = number(c, j, u)
                up = ladder[u][:, 0, :].bitcast(BF16)
                down = ladder[u][:, 1, :].bitcast(BF16)
                a, b, e, d = (t[:, :] for t in deq)
                V = [float(np.float32(v)) for v in NF4]
                ts, tt, stt = nc.vector.tensor_scalar, nc.vector.tensor_tensor, nc.vector.scalar_tensor_tensor

                def after(k):
                    dve.wait_ge(s_dq, n * DEQ_OPS + k + 1)

                def tell(ins):
                    ins.then_inc(s_dq, 1)

                dve.wait_ge(s_ladder, 2 + n + 1)
                dve.wait_ge(s_piece, 2 + n)
                tell(ts(a, up, rung(14), V[13], ALU.mult, ALU.max))
                tell(ts(b, up, rung(12), V[11], ALU.mult, ALU.max))
                tell(ts(e, down, rung(0), V[1], ALU.mult, ALU.min))
                tell(ts(d, down, rung(2), V[3], ALU.mult, ALU.min))
                after(1)
                tell(stt(a, a, V[15], b, ALU.min, ALU.min))
                after(3)
                tell(tt(e, e, d, ALU.max))
                if early:
                    between()
                after(4)
                tell(ts(b, up, rung(10), V[9], ALU.mult, ALU.max))
                after(5)
                tell(ts(d, down, rung(4), V[5], ALU.mult, ALU.min))
                after(6)
                tell(tt(a, a, b, ALU.min))
                after(7)
                tell(tt(e, e, d, ALU.max))
                after(9)
                tell(stt(e, down, rung(6), e, ALU.mult, ALU.max))
                if not early:
                    between()
                after(10)
                tell(stt(e, up, rung(8), e, ALU.mult, ALU.add))
                after(11)
                tell(tt(a, a, e, ALU.min))
                after(12)
                dve.wait_ge(s_tr1, n + 1)
                tt(wq_nat[u][:, :].rearrange("p (q e) -> p q e", e=QBLOCK),
                   a.rearrange("p (q e) -> p q e", e=QBLOCK),
                   absm[:, O0[c] // P + u, bass.ds(j * (QD // QBLOCK), QD // QBLOCK)].unsqueeze(2)
                   .to_broadcast([P, QD // QBLOCK, QBLOCK]), ALU.mult).then_inc(s_piece, 1)

            def piece_lo(c, j, u):
                dve.wait_ge(s_qhi, number(c, j, u) + 1)
                hi = wqt_part(c, HI, j, u)
                nc.vector.tensor_tensor(wqt_part(c, LO, j, u), tr1[u][:, :].rearrange("p (t o) -> p t o", t=DT),
                                        hi.bitcast(F32), ALU.subtract).then_inc(s_qlo, 1)

            def piece_step(c, j, u, early=False):
                nxt = piece_at(c, j, u, 1)
                if nxt:
                    dequantise(*nxt, lambda: piece_lo(c, j, u), early)
                else:
                    piece_lo(c, j, u)

            dve.wait_ge(s_absm, 16)
            dequantise(0, 0, 0)
            dve.wait_ge(s_small, 48)
            dve.wait_ge(s_const, 64)
            link(nc.vector.tensor_copy(ids_f[:, :], ids_i[:, :]))
            link(nc.vector.tensor_scalar(ids_w[:, :], ids_f[:, :], 0.0, float(NA), ALU.is_lt, ALU.mult))
            link(nc.vector.tensor_tensor(ids_w[:, :], ids_w[:, :], ids_f[:, :], ALU.add))
            link(nc.vector.tensor_scalar(ids_w[:, :], ids_w[:, :], 0.0, float(NA - 1), ALU.max, ALU.min))
            link(nc.vector.tensor_scalar(hit[:, :], ids_w[:, :], adapt_c[:, 0:1], None, ALU.is_equal))
            link(nc.vector.tensor_tensor(sel[:, :, :], hit[:, :].unsqueeze(2).to_broadcast([P, NB, R]),
                                         rank_c[:, :].unsqueeze(1).to_broadcast([P, NB, R]), ALU.mult))
            link(nc.vector.tensor_scalar(sel_s[:, :, :], sel[:, :, :], scale_c[:, 0:1], None, ALU.mult))
            dve.wait_ge(s_b1hi, 1)
            nc.vector.tensor_tensor(b1_hl[:, :, LO], b1_nat[:, :], b1_hl[:, :, HI].bitcast(F32),
                                    ALU.subtract).then_inc(s_b1, 1)

            def select_a():
                for q in range(4):
                    dve.wait_ge(s_a_hi, q + 1)
                    nc.vector.tensor_tensor(a_sel[:, :, q * 4:(q + 1) * 4, LO, :].rearrange("p b k r -> p k b r"),
                                            a_ps[q][:, :].rearrange("p (k b r) -> p k b r", k=4, b=NB),
                                            a_sel[:, :, q * 4:(q + 1) * 4, HI, :].rearrange("p b k r -> p k b r"),
                                            ALU.subtract).then_inc(s_a_lo, 1)

            for j in range(NJ):
                for u in range(OT[0]):
                    piece_step(0, j, u, early=u == OT[0] - 1)

            def slot_lo(pp, j, bank):
                dve.wait_ge(s_xhi, pp * KT + j + 1)
                nc.vector.tensor_tensor(x_t[:, j, LO, :], bank[:, 0:PT], x_t[:, j, HI, :].bitcast(F32),
                                        ALU.subtract).then_inc(s_xlo, 1)

            def first_lo(t):
                for j in FIRST_SLOTS.get(t, ()):
                    slot_lo(0, j, tr_first[j % 3])

            for c in range(NCH):
                n = CHUNKS[c]

                def step(j, u):
                    piece = piece_of_step(c, j, u)
                    if piece:
                        piece_step(*piece)

                if c < LAST:
                    groups(dve, c, step, select_a)
                else:
                    select_a()
                    for t in range(KT + 1):
                        first_lo(t)
                dve.wait_ge(s_bias2, 16 * (c + 1))
                dve.wait_ge(s_evac1, 2 + STEPS * (c + 1))
                nc.vector.tensor_tensor(bt_sb[0:1, 0:n], bt_sb[0:1, 0:n], bias2_sb[:, 0:n], ALU.add
                                        ).then_inc(s_btadd, 1)
                if c == LAST:
                    first_lo(KT + 1)
                dve.wait_ge(s_bthi, c + 1)
                nc.vector.tensor_tensor(bt_hl[LO][:, 0:n], bt_sb[:, 0:n], bt_hl[HI][:, 0:n],
                                        ALU.subtract).then_inc(s_glo, 1)
                dve.wait_ge(s_ghi, c + 1)
                nc.vector.tensor_tensor(g_hl[LO][:, 0:n], g_ps[:, 0:n], g_hl[HI][:, 0:n],
                                        ALU.subtract).then_inc(s_glo, 1)

            def loaded_lo(pp, j):
                dve.wait_ge(s_xhi, pp * KT + j + 1)
                nc.vector.tensor_tensor(x_t[:, j, LO, :], x_t[:, j, LO, :].bitcast(F32),
                                        x_t[:, j, HI, :].bitcast(F32), ALU.subtract).then_inc(s_xlo, 1)

            def pair_lo(h, b, w, mode):
                pp = (h * NB + b) * 2 + w
                for t in range(KT):
                    if h and t == 0:
                        dve.wait_ge(s_xa[w], 16 * (NB + b + 1))
                    if t == KT - 1:
                        for k in range(ACC):
                            u, q = divmod(k, NO)
                            dve.wait_ge(s_acc, ACC * pp + k + 1)
                            res = x_nat[w][:, u, COL[h] + q * 512:COL[h] + (q + 1) * 512]
                            nc.vector.tensor_tensor(res, acc2[k][:, :], res, ALU.add).then_inc(s_evac2, 1)
                    if t == RESTACK_STEP and h == 0:
                        dve.wait_ge(s_lsthi, pp + 1)
                        rows = slice(2 * R, 3 * R)
                        nc.vector.tensor_tensor(low_st[rows, :], rst_ps[rows, 0:PT],
                                                low_st[rows, :].bitcast(F32), ALU.subtract).then_inc(s_lst, 1)
                    if mode == MAKE:
                        for j in TURN.get(t, ()):
                            slot_lo(pp + 1, j, tr2[j % 2])
                    if mode == LOAD and 3 <= t:
                        loaded_lo(pp + 1, t - 3)
                if mode == LOAD:
                    for j in range(KT - 3, KT):
                        loaded_lo(pp + 1, j)

            with dve.Fori(0, NB - 1) as b:
                for w in range(2):
                    pair_lo(0, b, w, MAKE)
            pair_lo(0, NB - 1, 0, MAKE)
            pair_lo(0, NB - 1, 1, LOAD)
            with dve.Fori(0, NB - 1) as b:
                for w in range(2):
                    pair_lo(1, b, w, LOAD)
            pair_lo(1, NB - 1, 0, LOAD)
            pair_lo(1, NB - 1, 1, None)

        @block.tensor
        def _(pe):
            def select_a():
                pe.wait_ge(s_a_nat, 16)
                for q in range(4):
                    for t in range(4):
                        i = 4 * q + t
                        last = nc.tensor.matmul(a_ps[q][:, t * P:(t + 1) * P], a_nat[:, i * P:(i + 1) * P],
                                                sel[:, :, :].rearrange("p b r -> p (b r)"), start=True, stop=True)
                    last.then_inc(s_a_mm, 1)

            pe.wait_ge(s_const, 64)
            def transpose_piece(c, j, u):
                n = number(c, j, u)
                pe.wait_ge(s_piece, 2 + n + 1)
                pe.wait_ge(s_qlo, n + 1)
                for t in range(DT):
                    last = nc.tensor.transpose(tr1[u][:, t * P:(t + 1) * P], wq_nat[u][:, t * P:(t + 1) * P],
                                               ident[:, :])
                last.then_inc(s_tr1, 1)

            def three(out_ap, hi_t, lo_t, hi_m, lo_m, first, last, **kw):
                nc.tensor.matmul(out_ap, hi_t, hi_m, start=first, stop=False, **kw)
                nc.tensor.matmul(out_ap, hi_t, lo_m, start=False, stop=False, **kw)
                return nc.tensor.matmul(out_ap, lo_t, hi_m, start=False, stop=last, **kw)

            def transpose_slot(pp, w, j, bank):
                for u in range(2):
                    last = nc.tensor.transpose(bank[:, u * P:(u + 1) * P], x_nat[w][:, u, j * P:(j + 1) * P],
                                               ident[:, :])
                last.then_inc(s_tr2, 1)

            def first_slots(t):
                for j in FIRST_SLOTS.get(t, ()):
                    if j == 0:
                        pe.wait_ge(s_xa[0], 16)
                        pe.wait_ge(s_a_lo, 4)
                    if j == KT // 2:
                        pe.wait_ge(s_xb[0], 16)
                    if j >= 3:
                        pe.wait_ge(s_xlo, j)
                    transpose_slot(0, 0, j, tr_first[j % 3])

            n = CHUNKS[0]
            for s in range(BLOCKS):
                q, half = divmod(s, 2)
                if s == 0:
                    for u in range(OT[0]):
                        transpose_piece(0, 0, u)
                if half == 0:
                    pe.wait_ge(s_qlo, 2 + OT[0] * (q + 1))
                pe.wait_ge(s_wlo, 4 + 2 * (s + 1))
                t = w_hl[s % 2]
                for u in range(UT):
                    i = half * UT + u
                    odd = i % 2
                    acc = block_ps[i // 2][:, odd * n:(odd + 1) * n]
                    for k in range(DT):
                        w_k, q_k = k * UT + u, q * DT + k
                        last = three(acc, t[:, HI, w_k, :], t[:, LO, w_k, :], wq_t[0][:, HI, q_k, 0:n],
                                     wq_t[0][:, LO, q_k, 0:n], q == 0 and k == 0 and not odd,
                                     q == NJ - 1 and k == DT - 1, skip_group_check=True)
                last.then_inc(s_mm1, 1)
                if q + 1 < NJ:
                    transpose_piece(0, q + 1, half)

            pe.wait_ge(s_b1, 1)
            for c in range(NCH):
                n = CHUNKS[c]
                wq = wq_t[c % 2]
                pe.wait_ge(s_qlo, 2 + PIECE0[c + 1])

                def tile_products(u, s):
                    par = (TILES * c + u) % 2
                    pe.wait_ge(s_wlo, 4 + 2 * (TILES * c + s) + 2)
                    pe.wait_ge(s_evac1, STEPS * c + s + 1)
                    t = w_hl[par]
                    for k in range(KT):
                        last = three(acc1[u % 2][:, 0:n], t[:, HI, k, :], t[:, LO, k, :],
                                     wq[:, HI, k, 0:n], wq[:, LO, k, 0:n], k == 0, k == KT - 1)
                    last.then_inc(s_mm1, 1)

                def step(j, u):
                    tile_products(u, j * UT + u)
                    piece = piece_of_step(c, j, u)
                    if piece:
                        transpose_piece(*piece)
                    if c == LAST and isinstance(j, int):
                        first_slots(j * UT + u)

                if c == LAST:
                    groups(pe, c, step, select_a)
                else:
                    with pe.Fori(BLOCKS // UT if c == 0 else 0, NJ) as j:
                        for u in range(UT):
                            step(j, u)
                tile_products(KT, KT)
                if c == LAST:
                    first_slots(KT)
                pe.wait_ge(s_evac1, STEPS * c + KT + 2)
                for k in range(KT):
                    nc.tensor.matmul(acc1[1][0:2, 0:n], b1_hl[:, k, :], wq[:, HI, k, 0:n],
                                     start=(k == 0), stop=False)
                    last = nc.tensor.matmul(acc1[1][0:2, 0:n], b1_hl[:, k, :], wq[:, LO, k, 0:n],
                                            start=False, stop=(k == KT - 1))
                last.then_inc(s_mm1, 1)
                if c == LAST:
                    first_slots(KT + 1)
                if c == 0:
                    pe.wait_ge(s_sel, 9)
                pe.wait_ge(s_evac1, 2 + STEPS * c + KT + 1)
                if c:
                    pe.wait_ge(s_glo, 2 * c)
                nc.tensor.matmul(g_ps[:, 0:n], sel_s[:, :, :].rearrange("p b r -> p (b r)"), v_sb[:, 0:n],
                                 start=True, stop=True).then_inc(s_gmm, 1)

            pe.wait_ge(s_evac1, 2 + STEPS * NCH)

            def pair_products(h, b, w, mode):
                v = h * NB + b
                pp = 2 * v + w
                for t in range(KT):
                    pe.wait_ge(s_xlo, 2 + pp * KT + t + 1)
                    pe.wait_ge(s_wtlo, h * KT + t + 1)
                    for k in range(2 * NO):
                        u, q = divmod(k, NO)
                        if t == 0:
                            pe.wait_ge(s_evac2, 4 * pp + k + 1)
                        tok, cols = slice(u * P, (u + 1) * P), slice(q * 512, (q + 1) * 512)
                        last = three(acc2[k][:, :], x_t[:, t, HI, tok], x_t[:, t, LO, tok],
                                     wt[:, PLACE[t], HI, cols], wt[:, PLACE[t], LO, cols], t == 0, t == KT - 1)
                        if t == KT - 1:
                            last.then_inc(s_acc, 1)
                    if t < KT - 1:
                        last.then_inc(s_step, 1)
                    if h == 0 and t in LOW_STEPS:
                        if t == LOW_STEPS[0]:
                            if w == 0:
                                pe.wait_ge(s_glo, 2 * NCH)
                            pe.wait_ge(s_ab, 16 * (v + 1))
                        for j in (2 * (t - 1), 2 * (t - 1) + 1):
                            pe.wait_ge(s_xlo, 2 + pp * KT + j + 1)
                            for hl in (HI, LO):
                                last = nc.tensor.matmul(low_ps[0:2 * R, 0:PT], a_b[:, j, :], x_t[:, j, hl, :],
                                                        start=(j == 0 and hl == HI),
                                                        stop=(j == KT - 1 and hl == LO))
                        if t == LOW_STEPS[-1]:
                            last.then_inc(s_low, 1)
                    if h == 0 and t == RESTACK_STEP:
                        pe.wait_ge(s_lowev, pp + 1)
                        nc.tensor.matmul(rst_ps[0:3 * R, 0:PT], rst[:, :], low_sb[:, :], start=True,
                                         stop=True).then_inc(s_rst, 1)
                    if t == LORA_STEP:
                        if h == 0:
                            pe.wait_ge(s_lst, pp + 1)
                        else:
                            pe.wait_ge(s_lowld, 16 * (pp - PAIRS + 1))
                        pe.wait_ge(s_gb, 5 * 16 * (v + 1))
                        for k in range(2 * NO):
                            u, q = divmod(k, NO)
                            last = nc.tensor.matmul(acc2[k][:, :], low_st[:, u * P:(u + 1) * P],
                                                    g_b[:, q * 512:(q + 1) * 512], start=False, stop=False)
                        last.then_inc(s_lora, 1)
                    if mode == MAKE and t in TURN:
                        for j in TURN[t]:
                            if j == 0:
                                pe.wait_ge(s_xa[1 - w], 16 * (v + 1 + w))
                            if j == KT // 2:
                                pe.wait_ge(s_xb[1 - w], 16 * (v + 1 + w))
                            pe.wait_ge(s_xlo, (pp + 1) * KT + j + 1)
                            transpose_slot(pp + 1, 1 - w, j, tr2[j % 2])

            with pe.Fori(0, NB - 1) as b:
                for w in range(2):
                    pair_products(0, b, w, MAKE)
            pair_products(0, NB - 1, 0, MAKE)
            pair_products(0, NB - 1, 1, LOAD)
            with pe.Fori(0, NB) as b:
                for w in range(2):
                    pair_products(1, b, w, LOAD)


_INS = ['x', 'itok_B_1_7', 'L0_cond_weight', 'L0_cond_bias', 'L0_cond_lora_a_weights', 'L0_cond_lora_b_weights',
        'L0_cond_scaling_factors', 'L0_ffn_codes', 'L0_ffn_absmax', 'L0_ffn_bias']


def kernel(**inputs):
    import concourse.bacc as _bacc
    from concourse.bass_utils import run_bass_kernel_spmd as _run

    nc = _bacc.Bacc("TRN2", target_bir_lowering=False, num_devices=1)
    arrays, args = {}, []
    rows = np.arange(128)
    rank = inputs['L0_cond_lora_a_weights'].shape[1]
    consts = {
        'identity': np.eye(128, dtype=np.float32),
        'rank_of': (rows[:, None] % rank == np.arange(rank)[None, :]).astype(np.float32),
        'adapter_of': (rows[:, None] // rank).astype(np.float32),
        'restack': (np.arange(2 * rank)[:, None] % rank == np.arange(3 * rank)[None, :] % rank).astype(np.float32),
    }
    for name in _INS + list(consts):
        a = np.ascontiguousarray(inputs[name] if name in _INS else consts[name])
        arrays[f"in_{name}_dram"] = a
        args.append(nc.dram_tensor(f"in_{name}_dram", a.shape, mybir.dt.from_np(a.dtype), kind="ExternalInput").ap())
    shape = tuple(inputs['x'].shape)
    args.append(nc.dram_tensor("out_0_dram", shape, mybir.dt.float32, kind="ExternalOutput").ap())
    adaln_ffn_kernel(nc, *args)
    r = _run(nc, [arrays], core_ids=[0])
    return r.results[0]["out_0_dram"]
```
